# Optimizing a Trainium2 kernel written in Bass

```python
import numpy as np
import jax
import jax.numpy as jnp

def _softmax(x, axis=-1):
    return jax.nn.softmax(x, axis=axis)

def _gelu(x):
    return jax.nn.gelu(x, approximate=True)

def _silu(x):
    return jax.nn.silu(x)

def _sigmoid(x):
    return jax.nn.sigmoid(x)

def _layernorm(x, axis=-1, eps=1e-05):
    m = jnp.mean(x, axis=axis, keepdims=True)
    v = jnp.var(x, axis=axis, keepdims=True)
    return (x - m) / jnp.sqrt(v + eps)

def _scatter_add(tgt, idx, src, axis=0):
    return tgt.at[idx].add(src)

def _segment_sum(src, seg, n):
    return jax.ops.segment_sum(src, seg, n)
kernel_name = 'mk_prb_d1_jaxref_r8_b80a78'

def setup_inputs(seed: int=0):
    np.random.seed(seed)
    _w = jnp.asarray

    def _L0_attn_setup():
        import jax, jax.numpy as jnp
        import numpy as np
        B, N, D_IN, D_OUT = (4, 256, 128, 128)
        key = jax.random.key(seed)
        k = jax.random.split(key, 6)
        x = jax.random.normal(k[0], (B, N, D_IN), dtype=jnp.float32)
        sc_in = 1.0 / np.sqrt(D_IN)
        sc_out = 1.0 / np.sqrt(D_OUT)
        W_spin = jax.random.uniform(k[1], (D_OUT, D_IN), jnp.float32, -sc_in, sc_in)
        b_spin = jax.random.uniform(k[2], (D_OUT,), jnp.float32, -sc_in, sc_in)
        W_global = jax.random.uniform(k[3], (D_OUT, D_OUT), jnp.float32, -sc_out, sc_out)
        W_J = jax.random.uniform(k[4], (D_OUT, D_OUT), jnp.float32, -sc_out, sc_out)
        beta = jnp.ones((1,), dtype=jnp.float32)
        return {'x': x, 'W_spin': W_spin, 'b_spin': b_spin, 'W_global': W_global, 'W_J': W_J, 'beta': beta}
    _L0_attn_in = _L0_attn_setup()

    def _L0_ffn_setup():
        import jax, jax.numpy as jnp
        import numpy as np
        B, S, H = (1, 128, 128)
        E = 128
        NEXP = 16
        TOPK = 2
        ALPHA = 1.702
        LIMIT = 7.0

        def _moe_forward(x, Wg, bg, Wgu, bgu, Wd, bd):
            b, s, h = x.shape
            xt = x.reshape(-1, h)
            logits = xt @ Wg.T + bg
            top_vals, top_idx = jax.lax.top_k(logits, TOPK)
            rw = jax.nn.softmax(top_vals.astype(jnp.float32), axis=-1).astype(xt.dtype)
            onehot = jax.nn.one_hot(top_idx, NEXP, dtype=xt.dtype)
            cw = jnp.einsum('tk,tke->te', rw, onehot)
            gu = jnp.einsum('th,ehf->tef', xt, Wgu) + bgu[None]
            gate = gu[..., ::2]
            up = gu[..., 1::2]
            gate = jnp.minimum(gate, LIMIT)
            up = jnp.clip(up, -LIMIT, LIMIT)
            glu = gate * jax.nn.sigmoid(gate * ALPHA)
            gated = (up + 1.0) * glu
            out_e = jnp.einsum('tef,efh->teh', gated, Wd) + bd[None]
            out = jnp.einsum('teh,te->th', out_e, cw)
            return out.reshape(b, s, h)
        key = jax.random.key(seed)
        ks = jax.random.split(key, 8)
        hidden_states = jax.random.normal(ks[0], (B, S, H), dtype=jnp.float32)
        Wg = jax.random.normal(ks[1], (NEXP, H), dtype=jnp.float32) / np.sqrt(H)
        bg = jax.random.normal(ks[2], (NEXP,), dtype=jnp.float32) * 0.01
        Wgu = jax.random.normal(ks[3], (NEXP, H, 2 * E), dtype=jnp.float32) / np.sqrt(H)
        bgu = jax.random.normal(ks[4], (NEXP, 2 * E), dtype=jnp.float32) * 0.01
        Wd = jax.random.normal(ks[5], (NEXP, E, H), dtype=jnp.float32) / np.sqrt(E)
        bd = jax.random.normal(ks[6], (NEXP, H), dtype=jnp.float32) * 0.01
        return {'hidden_states': hidden_states, 'Wg': Wg, 'bg': bg, 'Wgu': Wgu, 'bgu': bgu, 'Wd': Wd, 'bd': bd}
    _L0_ffn_in = _L0_ffn_setup()
    _d = {'L0_attn_x': _L0_attn_in['x'], 'L0_attn_W_spin': _L0_attn_in['W_spin'], 'L0_attn_b_spin': _L0_attn_in['b_spin'], 'L0_attn_W_global': _L0_attn_in['W_global'], 'L0_attn_W_J': _L0_attn_in['W_J'], 'L0_attn_beta': _L0_attn_in['beta'], 'L0_ffn_Wg': _L0_ffn_in['Wg'], 'L0_ffn_bg': _L0_ffn_in['bg'], 'L0_ffn_Wgu': _L0_ffn_in['Wgu'], 'L0_ffn_bgu': _L0_ffn_in['bgu'], 'L0_ffn_Wd': _L0_ffn_in['Wd'], 'L0_ffn_bd': _L0_ffn_in['bd']}
    _x0 = _d['L0_attn_x']
    _d['L0_attn_x'] = jax.random.normal(jax.random.fold_in(jax.random.key(seed), 1), (2, 2048, 128), dtype=_x0.dtype)
    del _x0
    return _d

def reference(L0_attn_x, L0_attn_W_spin, L0_attn_b_spin, L0_attn_W_global, L0_attn_W_J, L0_attn_beta, L0_ffn_Wg, L0_ffn_bg, L0_ffn_Wgu, L0_ffn_bgu, L0_ffn_Wd, L0_ffn_bd):

    def _L0_attn_ref(x, W_spin, b_spin, W_global, W_J, beta):
        import jax, jax.numpy as jnp
        import numpy as np
        B, N, D_IN, D_OUT = (4, 256, 128, 128)
        s = jnp.einsum('bni,oi->bno', x, W_spin) + b_spin
        mean_field = jnp.mean(s, axis=1, keepdims=True)
        global_influence = jnp.einsum('bmd,od->bmo', mean_field, W_global)
        energy_fields = jnp.einsum('bnd,od->bno', s, W_J)
        scale = 1.0 / jnp.sqrt(jnp.float32(s.shape[2]))
        scores = jnp.einsum('bnd,bmd->bnm', energy_fields, s) * scale
        affinities = jax.nn.softmax(scores, axis=-1)
        local_field = jnp.einsum('bnm,bmd->bnd', affinities, s)
        return jnp.tanh(beta * (s + global_influence + local_field))

    def _L0_ffn_ref(hidden_states, Wg, bg, Wgu, bgu, Wd, bd):
        import jax, jax.numpy as jnp
        import numpy as np
        B, S, H = (1, 128, 128)
        E = 128
        NEXP = 16
        TOPK = 2
        ALPHA = 1.702
        LIMIT = 7.0

        def _moe_forward(x, Wg, bg, Wgu, bgu, Wd, bd):
            b, s, h = x.shape
            xt = x.reshape(-1, h)
            logits = xt @ Wg.T + bg
            top_vals, top_idx = jax.lax.top_k(logits, TOPK)
            rw = jax.nn.softmax(top_vals.astype(jnp.float32), axis=-1).astype(xt.dtype)
            onehot = jax.nn.one_hot(top_idx, NEXP, dtype=xt.dtype)
            cw = jnp.einsum('tk,tke->te', rw, onehot)
            gu = jnp.einsum('th,ehf->tef', xt, Wgu) + bgu[None]
            gate = gu[..., ::2]
            up = gu[..., 1::2]
            gate = jnp.minimum(gate, LIMIT)
            up = jnp.clip(up, -LIMIT, LIMIT)
            glu = gate * jax.nn.sigmoid(gate * ALPHA)
            gated = (up + 1.0) * glu
            out_e = jnp.einsum('tef,efh->teh', gated, Wd) + bd[None]
            out = jnp.einsum('teh,te->th', out_e, cw)
            return out.reshape(b, s, h)
        return _moe_forward(hidden_states, Wg, bg, Wgu, bgu, Wd, bd)
    x = L0_attn_x
    xn = _layernorm(x, axis=-1)
    x = x + _L0_attn_ref(xn, L0_attn_W_spin, L0_attn_b_spin, L0_attn_W_global, L0_attn_W_J, L0_attn_beta) + _L0_ffn_ref(xn, L0_ffn_Wg, L0_ffn_bg, L0_ffn_Wgu, L0_ffn_bgu, L0_ffn_Wd, L0_ffn_bd)
    return x

_drawn_inputs = setup_inputs


def setup_inputs(seed=0):
    import zlib

    import numpy as np

    out = dict(_drawn_inputs(seed))
    spreads = {}
    factors = {'L0_attn_W_global': 2.949, 'L0_attn_W_J': 5.979, 'L0_ffn_bgu': 8.0, 'L0_ffn_bd': 8.0}
    for name, (base, spread) in spreads.items():
        noise = np.random.default_rng([zlib.crc32(name.encode()), seed]).standard_normal(out[name].shape)
        drawn = base * np.exp(spread * noise) if base else spread * noise
        out[name] = jnp.asarray(drawn.astype(out[name].dtype))
    for name, factor in factors.items():
        out[name] = (out[name] * factor).astype(out[name].dtype)
    return out
```

```python
from contextlib import ExitStack

import concourse.bass as bass
from concourse import mybir

F32 = mybir.dt.float32
F32R = mybir.dt.float32r
BF16 = mybir.dt.bfloat16
U32 = mybir.dt.uint32
I32 = mybir.dt.int32
ALU = mybir.AluOpType
ACT = mybir.ActivationFunctionType
AX = mybir.AxisListType

P = 128
EPS = 1e-5
LIMIT = 7.0
ALPHA = 1.702


def build(nc, x, W_spin, b_spin, W_global, W_J, beta, Wg, bg, Wgu, bgu, Wd, bd, out):
    NB, N, D = x.shape
    NE, _, F2 = Wgu.shape
    F = F2 // 2
    assert D == P and F == P and N % 512 == 0
    TB = N // P
    NT = NB * TB
    CB = TB // 4
    NCH = NT // 4
    NP = TB // 2
    NSLOT_TILES = 2 * NT + NE
    NG = NSLOT_TILES // 4
    WC = F2 + D
    SCALE = 1.0 / float(D) ** 0.5
    BIG = 3.0e38
    assert NSLOT_TILES % 8 == 0 and NB == 2 and NE * NT == 512

    x_v = x.rearrange("b (p t) d -> b p t d", p=P)
    out_v = out.rearrange("b (p t) d -> b p t d", p=P)
    slots_x = nc.dram_tensor("slots_x", [NSLOT_TILES * P, D], F32, kind="Internal").ap()
    slots_y = nc.dram_tensor("slots_y", [NSLOT_TILES * P, D], F32, kind="Internal").ap()
    part = nc.dram_tensor("part", [P, TB, D], F32, kind="Internal").ap()
    bias_parts = nc.dram_tensor("bias_parts", [2, NE, WC], F32, kind="Internal").ap()
    slots_x_v = slots_x.rearrange("(s p) d -> p s d", p=P)
    slots_y_v = slots_y.rearrange("(s p) d -> p s d", p=P)

    with ExitStack() as ctx:
        def sb(name, shape, dt=F32):
            return ctx.enter_context(nc.sbuf_tensor(name, shape, dt))

        def ps(name, shape):
            return ctx.enter_context(nc.psum_tensor(name, shape, F32))

        def sem(name):
            return ctx.enter_context(nc.semaphore(name))

        xn = sb("xn", [P, NT, D])
        sTh, sTl = sb("sTh", [P, N], F32R), sb("sTl", [P, N], F32R)
        sh, sl = sb("sh", [P, TB, D], F32R), sb("sl", [P, TB, D], F32R)
        prob = sb("prob", [P, 2, N])
        pTh, pTl = sb("pTh", [P, TB, 2 * P], F32R), sb("pTl", [P, TB, 2 * P], F32R)
        wh, wl = sb("wh", [P, NE, WC], F32R), sb("wl", [P, NE, WC], F32R)
        wb = sb("wb", [P, NE, WC], F32R)
        xTh, xTl = sb("xTh", [P, 4, P], F32R), sb("xTl", [P, 4, P], F32R)
        gTh, gTl = sb("gTh", [P, 4, P], F32R), sb("gTl", [P, 4, P], F32R)
        eTh, eTl = sb("eTh", [P, 2 * P], F32R), sb("eTl", [P, 2 * P], F32R)
        oT = sb("oT", [P, 2 * P])
        gu_sb = sb("gu_sb", [P, 2, 2, 512])
        th = sb("th", [P, 512])
        xy = sb("xy", [P, 4, 4, D])
        sg = sb("sg", [P, 2, D])
        xb = sb("xb", [P, 2, D])
        rb = sb("rb", [P, 2, D])
        ident = sb("ident", [P, P])
        identr = sb("identr", [P, P], F32R)
        onesr = sb("onesr", [P, P], F32R)
        tri = sb("tri", [P, P], BF16)
        onesb = sb("onesb", [P, P], BF16)
        wspTh, wspTl = sb("wspTh", [P, P], F32R), sb("wspTl", [P, P], F32R)
        wjTh, wjTl = sb("wjTh", [P, P], F32R), sb("wjTl", [P, P], F32R)
        wglT = sb("wglT", [P, P])
        wgTh, wgTl = sb("wgTh", [P, NE], F32R), sb("wgTl", [P, NE], F32R)
        gb = sb("gb", [P, D])
        bspin = sb("bspin", [P, 1])
        betac = sb("betac", [P, 1])
        bgr = sb("bgr", [P, NE])
        mv = sb("mv", [P, TB, 2])
        rstd = sb("rstd", [P, TB])
        epsc = sb("epsc", [P, 1])
        msum = sb("msum", [P, CB + 1])
        mx4 = sb("mx4", [P, 2, 4])
        nmax = sb("nmax", [P, 2])
        dn = sb("dn", [P, NT, 4])
        den = sb("den", [P, 2])
        rden = sb("rden", [P, 2])
        iot = sb("iot", [P, NSLOT_TILES], I32)
        w12 = sb("w12", [P, 2, NT])
        posu = sb("posu", [P, 2, NT], U32)
        eidf, iotf = oT[0:1, 0:NSLOT_TILES], oT[0:1, NSLOT_TILES:2 * NSLOT_TILES]
        eid = sb("eid", [1, NSLOT_TILES], I32)
        mk = rb[:].rearrange("p a b -> p (a b)").rearrange("p (k t) -> p k t", t=NT)
        sgf = sg[:].rearrange("p a b -> p (a b)")
        small = sgf[:, 0:6 * NE].rearrange("p (k e) -> p k e", e=NE)
        rev, j128 = sgf[:, 6 * NE:7 * NE], sgf[:, 7 * NE:7 * NE + NT]
        stats = sgf[:, 7 * NE + NT:7 * NE + NT + 6 * TB].rearrange("p (t s) -> p t s", s=6)
        wgu_st = prob[:].rearrange("p a n -> p (a n)").rearrange("p (e f) -> p e f", e=NE)
        wd_st = xy[:].rearrange("p a b d -> p (a b d)").rearrange("p (e f) -> p e f", e=NE)
        w4_st = gu_sb[:, 0].rearrange("p a n -> p (a n)")[:, 0:4 * P].rearrange("p (a n) -> p a n", a=4)
        b_st = gu_sb[0:NE, 1].rearrange("p a n -> p (a n)")[:, 0:WC]
        b_ad = th[0:NE, 0:WC]

        S = ps("S", [P, 4, 512])
        T = ps("T", [P, 2, 512])
        O = ps("O", [P, 512])
        M = ps("M", [P, 512])

        ld_x = [sem("ld_x0"), sem("ld_x1")]
        ld_w, ld_gu, ld_d, ld_b = sem("ld_w"), sem("ld_gu"), sem("ld_d"), sem("ld_b")
        consts = sem("consts")
        zeroed = sem("zeroed")
        dchain = sem("dchain")
        rstd_in, rstd_mid = sem("rstd_in"), sem("rstd_mid")
        xn_ready = sem("xn_ready")
        wt_turned, wt_hi, wt_done = sem("wt_turned"), sem("wt_hi"), sem("wt_done")
        t_fill, t_hi, t_lo = sem("t_fill"), sem("t_hi"), sem("t_lo")
        m_fill, m_hi, m_lo = sem("m_fill"), sem("m_hi"), sem("m_lo")
        xT_used = sem("xT_used")
        log_done = sem("log_done")
        mean_ready, g_done, g_ready = sem("mean_ready"), sem("g_done"), sem("g_ready")
        dlt, exp_dlt = sem("dlt"), sem("exp_dlt")
        oh_ready, rank_done, routed = sem("oh_ready"), sem("rank_done"), sem("routed")
        w_hi, w_lo = sem("w_hi"), sem("w_lo")
        b_adj, b_hi, b_lo = sem("b_adj"), sem("b_hi"), sem("b_lo")
        wb_clear, b_out, b_in = sem("wb_clear"), sem("b_out"), sem("b_in")
        score_done = sem("score_done")
        max4 = sem("max4")
        max_ready = sem("max_ready")
        exp_done = sem("exp_done")
        pv_done, oT_ready, back_done = sem("pv_done"), sem("oT_ready"), sem("back_done")
        den_ready, pre_ready, tanh_ready = sem("den_ready"), sem("pre_ready"), sem("tanh_ready")
        sg_half, sg_ready = sem("sg_half"), sem("sg_ready")
        xb_in, xb_out, base_ready, fin_ready = sem("xb_in"), sem("xb_out"), sem("base_ready"), sem("fin_ready")
        rb_in, rb_out, rb_ready = sem("rb_in"), sem("rb_out"), sem("rb_ready")
        scat = sem("scat")
        gat_a, gat_b = sem("gat_a"), sem("gat_b")
        ffn_half = sem("ffn_half")
        xg_in = [sem("xg_in0"), sem("xg_in1")]
        y_out = [sem("y_out0"), sem("y_out1")]
        gu_done, gate_ready, up_ready, au_ready = sem("gu_done"), sem("gate_ready"), sem("up_ready"), sem("au_ready")
        th_ready, ga_ready, y_done, y_ready = sem("th_ready"), sem("ga_ready"), sem("y_done"), sem("y_ready")

        T_PRO = [0, 0]
        n = NCH + CB
        T_ATT = [n, 0]
        n += 4 * TB
        T_MOE = n
        n += 2 * NG
        T_PRO[1] = n
        n += 2 * CB
        T_ATT[1] = n
        M_PRO = [0, CB + NP]
        M_ATT = [CB, CB + NP + CB]

        def tiles_T(n):
            return T[:, n % 2].rearrange("p (a b) -> p a b", a=4)

        def bc(ap, shape, at):
            return ap.unsqueeze(at).broadcast_to(shape)

        block = ctx.enter_context(nc.Block())

        @block.sync
        def _(sp):
            with nc.allow_non_contiguous_dma(reason="small vectors"):
                for b in range(NB):
                    sp.dma_start(xn[:, b * TB:(b + 1) * TB], x_v[b]).then_inc(ld_x[b], 16)
                    if b == 0:
                        sp.dma_start(w4_st[:, 0], W_spin).then_inc(ld_w, 16)
                        sp.dma_start(w4_st[:, 1], W_J).then_inc(ld_w, 16)
                        sp.dma_start(w4_st[:, 2], W_global).then_inc(ld_w, 16)
                        sp.dma_start(w4_st[0:NE, 3], Wg).then_inc(ld_w, 16)
                        sp.dma_start(bspin[:], b_spin.unsqueeze(1)).then_inc(ld_w, 16)
                        sp.dma_start(betac[:], beta.partition_broadcast(P)).then_inc(ld_w, 16)
                        sp.dma_start(bgr[:], bg.partition_broadcast(P)).then_inc(ld_w, 16)
                        sp.dma_start(b_st[:, 0:F2], bgu).then_inc(ld_b, 16)
                        sp.dma_start(b_st[:, F2:WC], bd).then_inc(ld_b, 16)
                sp.dma_start(wd_st, Wd.rearrange("e k n -> k e n")).then_inc(ld_d, 16)
                sp.dma_start(wgu_st, Wgu.rearrange("e k n -> k e n")).then_inc(ld_gu, 16)
                sp.wait_ge(consts, 2)
                sp.dma_start(
                    slots_x.rearrange("(p r) d -> p (r d)", p=P).rearrange("p (a n) -> p a n", n=2 * D),
                    bc(xb[:].rearrange("p a d -> p (a d)"), [P, NSLOT_TILES // 2, 2 * D], 1)).then_inc(zeroed, 16)
                sp.wait_ge(b_hi, 1)
                sp.dma_start(bias_parts[0], pTh[0:NE].rearrange("p a b -> p (a b)")[:, 0:WC].bitcast(F32)).then_inc(b_out, 16)
                sp.wait_ge(b_lo, 1)
                sp.dma_start(bias_parts[1], pTl[0:NE].rearrange("p a b -> p (a b)")[:, 0:WC].bitcast(F32)).then_inc(b_out, 16)
                sp.wait_ge(b_out, 32)
                sp.wait_ge(wb_clear, 1)
                sp.dma_start(wb[0:2].bitcast(F32), bias_parts).then_inc(b_in, 16)
                sp.wait_ge(zeroed, 16)
                for k in range(NP):
                    if k:
                        sp.wait_ge(xb_out, k * 16)
                    sp.dma_start(xb[:], x_v[0][:, 2 * k:2 * k + 2]).then_inc(xb_in, 16)
                    sp.wait_ge(fin_ready, k + 1)
                    sp.dma_start(part[:, 2 * k:2 * k + 2], xb[:]).then_inc(xb_out, 16)
                sp.wait_ge(scat, 16 * 2 * NT)
                for u in range(2):
                    sp.dma_start(xy[:, u], slots_x_v[:, 4 * u:4 * u + 4]).then_inc(xg_in[u], 16)

                for j in range(NG // 2 - 1):
                    for u in range(2):
                        sp.wait_ge(gu_done, 2 * j + u + 1)
                        sp.dma_start(xy[:, u], slots_x_v[:, 8 * j + 8 + 4 * u:8 * j + 12 + 4 * u]).then_inc(xg_in[u], 16)
                for k in range(NP):
                    sp.wait_ge(xb_out, k * 16 + NP * 16)
                    sp.dma_start(xb[:], x_v[1][:, 2 * k:2 * k + 2]).then_inc(xb_in, 16)
                    if k:
                        sp.wait_ge(rb_out, k * 16)
                    sp.dma_start(rb[:], part[:, 2 * k:2 * k + 2]).then_inc(rb_in, 16)
                    sp.wait_ge(rb_ready, k + 1)
                    sp.dma_start(out_v[0][:, 2 * k:2 * k + 2], rb[:]).then_inc(rb_out, 16)
                    sp.wait_ge(fin_ready, k + 1 + NP)
                    sp.dma_start(out_v[1][:, 2 * k:2 * k + 2], xb[:]).then_inc(xb_out, 16)
                sp.wait_ge(xb_out, 2 * NP * 16)
                sp.wait_ge(rb_out, NP * 16)

        @block.gpsimd
        def _(pool):
            nc.gpsimd.memset(xb[:], 0.0).then_inc(consts, 1)
            nc.gpsimd.memset(ident[:], 0.0).then_inc(consts, 1)
            nc.gpsimd.memset(tri[:], 1.0).then_inc(consts, 1)
            nc.gpsimd.memset(onesb[:], 1.0).then_inc(consts, 1)
            nc.gpsimd.iota(iot[:], [[1, NSLOT_TILES]], base=0, channel_multiplier=0).then_inc(consts, 1)
            nc.gpsimd.memset(epsc[:], EPS).then_inc(consts, 1)
            nc.gpsimd.memset(onesr[:].bitcast(F32), 1.0).then_inc(consts, 1)
            pool.wait_ge(consts, 7)
            nc.gpsimd.affine_select(out=ident[:], in_=ident[:], compare_op=ALU.not_equal, fill=1.0, base=0,
                                    pattern=[[-1, P]], channel_multiplier=1).then_inc(consts, 1)
            nc.gpsimd.affine_select(out=tri[:], in_=tri[:], compare_op=ALU.is_gt, fill=0.0, base=0,
                                    pattern=[[1, P]], channel_multiplier=-1).then_inc(consts, 1)
            nc.gpsimd.memset(wb[:].bitcast(F32), 0.0).then_inc(wb_clear, 1)
            pool.wait_ge(zeroed, 16)
            pool.wait_ge(routed, 1)

            def fin(g):
                pool.wait_ge(tanh_ready, g + 1)
                if g < NP:
                    pool.wait_ge(xb_in, 16 * (g + 1))
                else:
                    pool.wait_ge(base_ready, g + 1 - NP)
                nc.gpsimd.tensor_tensor(xb[:], xb[:], sg[:], ALU.add).then_inc(fin_ready, 1)

            def sg_step(g):
                k = g % NP
                if g:
                    pool.wait_ge(fin_ready, g)
                if k == 0:
                    pool.wait_ge(t_lo, T_PRO[g // NP] + (NCH + CB if g == 0 else 2 * CB))
                    pool.wait_ge(g_ready, g // NP + 1)
                nc.gpsimd.tensor_tensor(sg[:], sh[:, 2 * k:2 * k + 2].bitcast(F32), sl[:, 2 * k:2 * k + 2].bitcast(F32),
                                        ALU.add).then_inc(sg_half, 1)
                pool.wait_ge(sg_half, g + 1)
                nc.gpsimd.tensor_tensor(sg[:], sg[:], bc(gb[:], [P, 2, D], 1), ALU.add).then_inc(sg_ready, 1)

            per = NT // NP
            for k in range(NP):
                sg_step(k)
                for t in range(per * k, per * k + per):
                    for c in range(2):
                        pool.indirect_dma_start(slots_x, bass.IndirectOffsetOnAxis(ap=posu[:, c, t:t + 1], axis=0),
                                                xn[:, t], None).then_inc(scat, 16)
                fin(k)
            with pool.Fori(0, NG // 2) as j:
                for u in range(2):
                    pool.wait_ge(y_ready, 2 * j + u + 1)
                    pool.dma_start(slots_y_v[:, bass.ds(8 * j + 4 * u, 4)], xy[:, 2 + u]).then_inc(y_out[u], 16)
            pool.wait_ge(y_out[0], 16 * (NG // 2))
            pool.wait_ge(y_out[1], 16 * (NG // 2))
            for k in range(NP):
                sg_step(NP + k)
                for side, (g_sem, t0) in enumerate(((gat_a, 2 * k), (gat_b, TB + 2 * k))):
                    if k:
                        pool.wait_ge(rb_ready if side == 0 else base_ready, k)
                    for t in range(2):
                        for c in range(2):
                            pool.indirect_dma_start(xy[:, side, 2 * t + c], None, slots_y,
                                                    bass.IndirectOffsetOnAxis(ap=posu[:, c, t0 + t:t0 + t + 1], axis=0),
                                                    ).then_inc(g_sem, 16)
                fin(NP + k)

        @block.tensor
        def _(pe):
            def three(o, ah, al, bh, bl, start=True, stop=True):
                nc.tensor.matmul(o, ah, bh, start=start, stop=False)
                nc.tensor.matmul(o, ah, bl, start=False, stop=False)
                return nc.tensor.matmul(o, al, bh, start=False, stop=stop)

            def t_free(n):
                if not isinstance(n, int) or n >= 2:
                    pe.wait_ge(t_lo, n - 1)

            def turn(n, tile, parity, ready=None):
                t_free(n)
                for a in range(4):
                    m = nc.tensor.transpose(T[:, parity, a * P:(a + 1) * P], tile(a), ident[:])
                m.then_inc(t_fill, 1)

            pe.wait_ge(consts, 9)
            pe.wait_ge(ld_w, 112)
            for a in range(3):
                nc.tensor.transpose(S[:, 0, a * P:(a + 1) * P], w4_st[:, a], ident[:])
            nc.tensor.transpose(S[:, 0, 3 * P:3 * P + NE], w4_st[0:NE, 3], ident[0:NE, 0:NE]).then_inc(wt_turned, 1)
            pe.wait_ge(wt_done, 1)
            pairs = ((xTh, xTl), (gTh, gTl))
            for c in range(NCH):
                pe.wait_ge(xn_ready, c + 1)
                turn(c, lambda a: xn[:, 4 * c + a], c % 2)
                pe.wait_ge(t_lo, c + 1)
                xh, xl = pairs[c % 2]
                for a in range(4):
                    m = three(S[:, 3, (4 * c + a) * NE:(4 * c + a + 1) * NE], xh[:, a], xl[:, a], wgTh[:], wgTl[:])
                if c < CB:
                    if c:
                        pe.wait_ge(m_lo, c)
                    three(M[:], wspTh[:], wspTl[:], xh[:].rearrange("p a b -> p (a b)"),
                          xl[:].rearrange("p a b -> p (a b)")).then_inc(m_fill, 1)
                else:
                    m.then_inc(log_done, 1)

            def s_rows(b, n0):
                for c in range(CB):
                    n = n0 + c
                    t_free(n)
                    pe.wait_ge(m_lo, M_PRO[b] + c + 1)
                    for a in range(4):
                        o = T[:, n % 2, a * P:(a + 1) * P]
                        nc.tensor.matmul(o, sTh[:, (4 * c + a) * P:(4 * c + a + 1) * P], identr[:], start=True, stop=False)
                        m = nc.tensor.matmul(o, sTl[:, (4 * c + a) * P:(4 * c + a + 1) * P], identr[:], start=False, stop=True)
                    m.then_inc(t_fill, 1)

            def global_row(b):
                pe.wait_ge(mean_ready, b + 1)
                nc.tensor.matmul(O[:, 0:D], mean_bc, wglT[:], start=True, stop=True).then_inc(g_done, 1)

            mean_bc = oT[:, 0:P]
            s_rows(0, NCH)
            global_row(0)
            pe.wait_ge(oh_ready, 1)
            ohb = th[:].bitcast(BF16)[:, 0:NT * NE]
            nc.tensor.matmul(S[:, 0], tri[:], ohb, start=True, stop=True)
            nc.tensor.matmul(S[:, 1], onesb[:], ohb, start=True, stop=True).then_inc(rank_done, 1)

            def scores(q, half):
                for j in range(4):
                    pe.wait_ge(exp_done, 4 * q - 4 + j + 1)
                    o = S[:, j]
                    e_h, e_l = eTh[:, half * P:(half + 1) * P], eTl[:, half * P:(half + 1) * P]
                    three(o, e_h, e_l, sTh[:, 512 * j:512 * j + 512], sTl[:, 512 * j:512 * j + 512]).then_inc(score_done, 1)

            def energy(b, i, m):
                pe.wait_ge(m_lo, m)
                lo, hi = sTl[:, bass.ds(i * 2 * P, 2 * P)], sTh[:, bass.ds(i * 2 * P, 2 * P)]
                three(M[:, 0:2 * P], wjTh[:], wjTl[:], hi, lo).then_inc(m_fill, 1)

            def turn_probs(q, half, n):
                for j in range(4):
                    t_free(n + j)
                    pe.wait_ge(exp_done, 4 * q + j + 1)
                    for a in range(4):
                        m = nc.tensor.transpose(T[:, j % 2, a * P:(a + 1) * P],
                                                prob[:, half, (4 * j + a) * P:(4 * j + a + 1) * P], ident[:])
                    m.then_inc(t_fill, 1)

            def values(g, n):
                if isinstance(g, int):
                    pe.wait_ge(pre_ready, g)
                for t in range(TB):
                    if t % 4 == 0:
                        pe.wait_ge(t_lo, n + t // 4 + 1)
                    m = three(O[:, 0:2 * P], sh[:, t], sl[:, t], pTh[:, t], pTl[:, t], start=t == 0, stop=t == TB - 1)
                m.then_inc(pv_done, 1)

            def turn_back(g):
                pe.wait_ge(oT_ready, g + 1)
                nc.tensor.transpose(O[:, 2 * P:3 * P], oT[:, 0:P], ident[:])
                nc.tensor.transpose(O[:, 3 * P:4 * P], oT[:, P:2 * P], ident[:]).then_inc(back_done, 1)

            def attention(b):
                q0, g0, n0, m0 = b * TB, b * NP, T_ATT[b], M_ATT[b]
                energy(b, 0, m0)
                pe.wait_ge(m_lo, m0 + 1)
                pe.wait_ge(g_ready, b + 1)
                if b == 0:
                    pe.wait_ge(routed, 1)
                else:
                    pe.wait_ge(up_ready, NG)
                scores_first(q0)
                scores(q0 + 1, 1)
                with pe.Fori(0, NP - 1) as i:
                    energy(b, i + 1, m0 + i + 1)
                    turn_probs(q0 + 2 * i, 0, n0 + 8 * i)
                    pe.wait_ge(m_lo, m0 + i + 2)
                    scores(q0 + 2 * i + 2, 0)
                    turn_probs(q0 + 2 * i + 1, 1, n0 + 8 * i + 4)
                    values(g0 + i, n0 + 8 * i + 4)
                    scores(q0 + 2 * i + 3, 1)
                    turn_back(g0 + i)
                i = NP - 1
                turn_probs(q0 + 2 * i, 0, n0 + 8 * i)
                turn_probs(q0 + 2 * i + 1, 1, n0 + 8 * i + 4)
                values(g0 + i, n0 + 8 * i + 4)
                turn_back(g0 + i)

            def scores_first(q):
                if q:
                    scores(q, 0)
                    return
                for j in range(4):
                    three(S[:, j], eTh[:, 0:P], eTl[:, 0:P], sTh[:, 512 * j:512 * j + 512],
                          sTl[:, 512 * j:512 * j + 512]).then_inc(score_done, 1)

            attention(0)

            def turn_slots(n, u, bank, count):
                pe.wait_ge(xg_in[u], count)
                turn(n, lambda a: xy[:, u, a], bank)

            def gate_up(g, u, n, idx):
                pe.wait_ge(t_lo, n + 1)
                if not (isinstance(g, int) and g < 2):
                    pe.wait_ge(up_ready, g - 1)
                for a in range(4):
                    e = pe.value_load(eid[0:1, idx(a)], min_val=0, max_val=NE - 1)
                    o = S[:, 2 * u + a // 2, (a % 2) * F2:(a % 2 + 1) * F2]
                    cols = bass.ds(e * WC, F2)
                    nc.tensor.matmul(o, onesr[:], wb2[:, cols], start=True, stop=False)
                    m = three(o, xTh[:, a], xTl[:, a], wh2[:, cols], wl2[:, cols], start=False)
                m.then_inc(gu_done, 1)

            def down(g, u, n, idx):
                pe.wait_ge(t_lo, n + 1)
                if not (isinstance(g, int) and g == 0):
                    pe.wait_ge(y_ready, g)
                bank = (O, M)[u]
                for a in range(4):
                    e = pe.value_load(eid[0:1, idx(a)], min_val=0, max_val=NE - 1)
                    cols = bass.ds(e * WC + F2, D)
                    o = bank[:, a * P:(a + 1) * P]
                    nc.tensor.matmul(o, onesr[:], wb2[:, cols], start=True, stop=False)
                    m = three(o, gTh[:, a], gTl[:, a], wh2[:, cols], wl2[:, cols], start=False)
                m.then_inc(y_done, 1)

            wh2, wl2, wb2 = (w[:].rearrange("p e n -> p (e n)") for w in (wh, wl, wb))
            pe.wait_ge(w_lo, 3)
            pe.wait_ge(b_in, 16)
            pe.wait_ge(pre_ready, NP)
            turn_slots(T_MOE, 0, 0, 16)
            gate_up(0, 0, T_MOE, lambda a: slice(a, a + 1))
            turn_slots(T_MOE + 1, 1, 1, 16)

            def expert_step(g, j, v, last=False):
                u = (v + 1) % 2
                n = T_MOE + 2 * g
                gate_up(g, u, n - 1, lambda a: bass.ds(4 * g + a, 1))
                turn_gated(g - 1, 1 - u, n, 0)
                if not last:
                    turn_slots(n + 1, 1 - u, 1, 16 * (j + 2))
                down(g - 1, 1 - u, n, lambda a: bass.ds(4 * g - 4 + a, 1))

            def turn_gated(g, u, n, bank):
                pe.wait_ge(ga_ready, g + 1)
                turn(n, lambda a: gu_sb[:, u, 1, a * P:(a + 1) * P], bank)

            expert_step(1, 0, 0)
            expert_step(2, 0, 1)
            with pe.Fori(1, NG // 2 - 1) as j:
                expert_step(2 * j + 1, j, 0)
                expert_step(2 * j + 2, j, 1)
            expert_step(NG - 1, NG // 2 - 1, 0, last=True)
            turn_gated(NG - 1, 1, T_MOE + 2 * NG - 1, 1)
            down(NG - 1, 1, T_MOE + 2 * NG - 1, lambda a: slice(4 * (NG - 1) + a, 4 * (NG - 1) + a + 1))

            for c in range(CB):
                turn(T_PRO[1] + c, lambda a: xn[:, TB + 4 * c + a], c % 2)
                pe.wait_ge(t_lo, T_PRO[1] + c + 1)
                xh, xl = pairs[c % 2]
                if c == 0:
                    pe.wait_ge(y_ready, NG)
                pe.wait_ge(m_lo, M_PRO[1] + c)
                three(M[:], wspTh[:], wspTl[:], xh[:].rearrange("p a b -> p (a b)"),
                      xl[:].rearrange("p a b -> p (a b)")).then_inc(m_fill, 1)
            s_rows(1, T_PRO[1] + CB)
            global_row(1)
            attention(1)

        @block.scalar
        def _(act):
            def hi(n, parity, dst, src=None):
                act.wait_ge(t_fill, n + 1)
                nc.scalar.activation(dst, T[:, parity].rearrange("p (a b) -> p a b", a=4), ACT.Copy).then_inc(t_hi, 1)

            act.wait_ge(consts, 9)
            nc.scalar.activation(identr[:], ident[:], ACT.Copy).then_inc(wt_hi, 1)
            act.wait_ge(rstd_in, 1)
            nc.scalar.activation(rstd[:], mv[:, :, 1], ACT.Sqrt, bias=epsc[:]).then_inc(rstd_mid, 1)
            act.wait_ge(wt_turned, 1)
            nc.scalar.activation(wspTh[:], S[:, 0, 0:P], ACT.Copy).then_inc(wt_hi, 1)
            nc.scalar.activation(wjTh[:], S[:, 0, P:2 * P], ACT.Copy).then_inc(wt_hi, 1)
            nc.scalar.activation(wglT[:], S[:, 0, 2 * P:3 * P], ACT.Copy).then_inc(wt_hi, 1)
            nc.scalar.activation(wgTh[:], S[:, 0, 3 * P:3 * P + NE], ACT.Copy).then_inc(wt_hi, 1)

            def spin_hi(b, c):
                act.wait_ge(m_fill, M_PRO[b] + c + 1)
                nc.scalar.activation(sTh[:, 512 * c:512 * c + 512], M[:], ACT.Identity, bias=bspin[:],
                                     accum_out=msum[:, c:c + 1]).then_inc(m_hi, 1)

            bufs = (xTh, gTh)
            for c in range(NCH):
                if c >= 2:
                    if c - 2 < CB:
                        act.wait_ge(m_fill, c - 1)
                    else:
                        act.wait_ge(log_done, c - 1 - CB)
                hi(c, c % 2, bufs[c % 2][:])
                if c < CB:
                    spin_hi(0, c)
                if c == CB - 1:
                    act.wait_ge(rstd_in, 2)
                    nc.scalar.activation(rstd[:], mv[:, :, 1], ACT.Sqrt, bias=epsc[:]).then_inc(rstd_mid, 1)
                    act.wait_ge(b_adj, 1)
                    nc.scalar.activation(pTh[0:NE].rearrange("p a b -> p (a b)")[:, 0:WC], b_ad, ACT.Copy).then_inc(b_hi, 1)
                if c == 4:
                    act.wait_ge(ld_d, 16)
                    nc.scalar.activation(wh[:, :, F2:WC], wd_st, ACT.Copy, scale=0.5).then_inc(w_hi, 1)
                if c == 5:
                    act.wait_ge(ld_gu, 16)
                    for s in range(2):
                        nc.scalar.activation(wh[:, :, s * F:(s + 1) * F],
                                             wgu_st.rearrange("p e (f s) -> p s e f", s=2)[:, s], ACT.Copy).then_inc(w_hi, 1)
            for c in range(CB):
                hi(NCH + c, c % 2, sh[:, 4 * c:4 * c + 4])
            act.wait_ge(g_done, 1)
            nc.scalar.activation(gb[:], O[:, 0:D], ACT.Copy).then_inc(g_ready, 1)
            act.wait_ge(dlt, 1)
            nc.scalar.activation(mk[:, 5], mk[:, 4], ACT.Exp).then_inc(exp_dlt, 1)

            def energy_hi(m, scores_seen):
                act.wait_ge(m_fill, m + 1)
                act.wait_ge(score_done, scores_seen)
                nc.scalar.activation(eTh[:], M[:, 0:2 * P], ACT.Copy, scale=SCALE).then_inc(m_hi, 1)

            def exps(q, half, used):
                act.wait_ge(max_ready, q + 1)
                act.wait_ge(t_fill, used)
                for j in range(4):
                    nc.scalar.activation(prob[:, half, 512 * j:512 * j + 512], S[:, j], ACT.Exp, bias=nmax[:, half:half + 1],
                                         accum_out=dn2[:, bass.ds(4 * q + j, 1)]).then_inc(exp_done, 1)

            dn2 = dn[:].rearrange("p t j -> p (t j)")

            def probs_hi(n, half):
                for j in range(4):
                    hi(n + j, j % 2, pTh[:, 4 * j:4 * j + 4, half * P:(half + 1) * P])

            def out_T(g):
                act.wait_ge(pv_done, g + 1)
                nc.scalar.activation(oT[:], O[:, 0:2 * P], ACT.Copy).then_inc(oT_ready, 1)

            def tanh_step(g):
                act.wait_ge(pre_ready, g + 1)
                nc.scalar.activation(sg[:], sg[:], ACT.Tanh, scale=betac[:]).then_inc(tanh_ready, 1)

            def attention(b):
                q0, g0, n0, m0 = b * TB, b * NP, T_ATT[b], M_ATT[b]
                if b == 0:
                    act.wait_ge(w_lo, 3)
                    act.wait_ge(b_out, 32)
                energy_hi(m0, 4 * q0)
                exps(q0, 0, n0)
                exps(q0 + 1, 1, n0)
                with act.Fori(0, NP - 1) as i:
                    energy_hi(m0 + i + 1, 4 * q0 + 8 * i + 8)
                    probs_hi(n0 + 8 * i, 0)
                    exps(q0 + 2 * i + 2, 0, n0 + 8 * i + 4)
                    probs_hi(n0 + 8 * i + 4, 1)
                    out_T(g0 + i)
                    exps(q0 + 2 * i + 3, 1, n0 + 8 * i + 8)
                    tanh_step(g0 + i)
                i = NP - 1
                probs_hi(n0 + 8 * i, 0)
                probs_hi(n0 + 8 * i + 4, 1)
                out_T(g0 + i)
                tanh_step(g0 + i)

            attention(0)

            def rows_hi(n, u, g):
                if not (isinstance(g, int) and g == 0):
                    act.wait_ge(gu_done, g)
                hi(n, u, xTh[:])

            def gated_hi(n, g):
                if not (isinstance(g, int) and g == 0):
                    act.wait_ge(y_done, g)
                hi(n, 0, gTh[:])

            def sigmoid_half(g, u):
                act.wait_ge(gate_ready, g + 1)
                if not (isinstance(g, int) and g == 0):
                    act.wait_ge(ga_ready, g)
                nc.scalar.activation(th[:], gu_sb[:, u, 0], ACT.Tanh, scale=ALPHA / 2).then_inc(th_ready, 1)

            def y_copy(g, u, stored):
                act.wait_ge(y_done, g + 1)
                if not (isinstance(stored, int) and stored == 0):
                    act.wait_ge(y_out[u], stored)
                nc.scalar.activation(xy[:, 2 + u], (O, M)[u][:].rearrange("p (a d) -> p a d", a=4),
                                     ACT.Copy).then_inc(y_ready, 1)

            act.wait_ge(routed, 1)
            rows_hi(T_MOE, 0, 0)
            sigmoid_half(0, 0)
            rows_hi(T_MOE + 1, 1, 1)

            def expert_step(g, j, v, last=False):
                u = (v + 1) % 2
                n = T_MOE + 2 * g
                sigmoid_half(g, u)
                gated_hi(n, g - 1)
                if not last:
                    rows_hi(n + 1, 1, g + 1)
                y_copy(g - 1, 1 - u, 16 * j)

            expert_step(1, 0, 0)
            expert_step(2, 0, 1)
            with act.Fori(1, NG // 2 - 1) as j:
                expert_step(2 * j + 1, j, 0)
                expert_step(2 * j + 2, j, 1)
            expert_step(NG - 1, NG // 2 - 1, 0, last=True)
            act.wait_ge(y_done, NG - 1)
            act.wait_ge(t_fill, T_MOE + 2 * NG)
            nc.scalar.activation(gTh[:], T[:, 1].rearrange("p (a b) -> p a b", a=4), ACT.Copy).then_inc(t_hi, 1)
            y_copy(NG - 1, 1, 16 * (NG // 2 - 1))

            for c in range(CB):
                if c >= 2:
                    act.wait_ge(m_fill, M_PRO[1] + c - 1)
                else:
                    act.wait_ge(y_done, NG)
                hi(T_PRO[1] + c, c % 2, bufs[c % 2][:])
                spin_hi(1, c)
            act.wait_ge(sg_ready, NP)
            for c in range(CB):
                hi(T_PRO[1] + CB + c, c % 2, sh[:, 4 * c:4 * c + 4])
            act.wait_ge(g_done, 2)
            nc.scalar.activation(gb[:], O[:, 0:D], ACT.Copy).then_inc(g_ready, 1)
            attention(1)

        @block.vector
        def _(dve):
            v = nc.vector
            count = [0]

            def link(ins):
                count[0] += 1
                ins.then_inc(dchain, 1)
                dve.wait_ge(dchain, count[0])

            def lo(n, parity, dst, high):
                dve.wait_ge(t_hi, n + 1)
                v.tensor_tensor(dst, T[:, parity].rearrange("p (a b) -> p a b", a=4), high.bitcast(F32),
                                ALU.subtract).then_inc(t_lo, 1)

            def spin_lo(b, c):
                dve.wait_ge(m_hi, M_PRO[b] + c + 1)
                v.scalar_tensor_tensor(out=sTl[:, 512 * c:512 * c + 512], in0=M[:], scalar=bspin[:],
                                       in1=sTh[:, 512 * c:512 * c + 512].bitcast(F32), op0=ALU.add,
                                       op1=ALU.subtract).then_inc(m_lo, 1)

            def mean_step(b):
                dve.wait_ge(m_hi, M_PRO[b] + CB)
                link(v.tensor_reduce(msum[:, CB:CB + 1], msum[:, 0:CB], AX.X, ALU.add))
                link(v.tensor_scalar(msum[:, CB:CB + 1], msum[:, CB:CB + 1], 1.0 / N, None, ALU.mult))
                v.tensor_scalar(oT[:, 0:P], ident[:], 0.0, msum[:, CB:CB + 1], ALU.mult, ALU.add).then_inc(mean_ready, 1)

            def normalise(b):
                dve.wait_ge(ld_x[b], 16)
                for t in range(TB):
                    ins = v.bn_stats(stats[:, t], xn[:, b * TB + t])
                link(ins)
                for t in range(TB):
                    ins = v.bn_aggr(mv[:, t], stats[:, t])
                ins.then_inc(rstd_in, 1)
                dve.wait_ge(rstd_mid, b + 1)
                link(v.reciprocal(rstd[:], rstd[:]))
                for t in range(TB):
                    ins = v.tensor_scalar(xn[:, b * TB + t], xn[:, b * TB + t], mv[:, t, 0:1], rstd[:, t:t + 1],
                                          ALU.subtract, ALU.mult)
                    if t % 4 == 3:
                        ins.then_inc(xn_ready, 1)

            normalise(0)
            dve.wait_ge(wt_hi, 5)
            v.tensor_tensor(wspTl[:], S[:, 0, 0:P], wspTh[:].bitcast(F32), ALU.subtract)
            v.tensor_tensor(wjTl[:], S[:, 0, P:2 * P], wjTh[:].bitcast(F32), ALU.subtract)
            v.tensor_tensor(wgTl[:], S[:, 0, 3 * P:3 * P + NE], wgTh[:].bitcast(F32), ALU.subtract).then_inc(wt_done, 1)
            dve.wait_ge(ld_b, 32)
            bt = b_st[:, 0:F2].rearrange("p (f s) -> p s f", s=2)
            v.tensor_copy(b_ad[:, 0:F], bt[:, 0])
            v.tensor_scalar(b_ad[:, F:F2], bt[:, 1], 1.0, None, ALU.add)
            v.tensor_copy(b_ad[:, F2:WC], b_st[:, F2:WC]).then_inc(b_adj, 1)
            bufs = ((xTh, xTl), (gTh, gTl))
            for c in range(NCH):
                if c >= 2:
                    if c - 2 < CB:
                        dve.wait_ge(m_fill, c - 1)
                    else:
                        dve.wait_ge(log_done, c - 1 - CB)
                lo(c, c % 2, bufs[c % 2][1][:], bufs[c % 2][0][:])
                if c < CB:
                    spin_lo(0, c)
                if c == CB - 1:
                    normalise(1)
            mean_step(0)
            for c in range(CB):
                lo(NCH + c, c % 2, sl[:, 4 * c:4 * c + 4], sh[:, 4 * c:4 * c + 4])
            dve.wait_ge(b_hi, 1)
            flat_h, flat_l = (w[0:NE].rearrange("p a b -> p (a b)")[:, 0:WC] for w in (pTh, pTl))
            v.tensor_tensor(flat_l, b_ad, flat_h.bitcast(F32), ALU.subtract).then_inc(b_lo, 1)
            dve.wait_ge(w_hi, 1)
            v.scalar_tensor_tensor(out=wl[:, :, F2:WC], in0=wd_st, scalar=0.5, in1=wh[:, :, F2:WC].bitcast(F32),
                                   op0=ALU.mult, op1=ALU.subtract).then_inc(w_lo, 1)
            dve.wait_ge(w_hi, 3)
            for s in range(2):
                v.tensor_tensor(wl[:, :, s * F:(s + 1) * F], wgu_st.rearrange("p e (f s) -> p s e f", s=2)[:, s],
                                wh[:, :, s * F:(s + 1) * F].bitcast(F32), ALU.subtract).then_inc(w_lo, 1)

            sh3 = [P, NT, NE]
            buf = [gu_sb[:, a, c].rearrange("p (t e) -> p t e", t=NT) for a in range(2) for c in range(2)]
            buf += [xy[:, a].rearrange("p b d -> p (b d)").rearrange("p (t e) -> p t e", t=NT) for a in range(4)]
            L, KEY, OH1, OH2, A, B_, C, MASK = buf
            dve.wait_ge(log_done, NCH - CB)
            dve.wait_ge(ld_w, 112)
            dve.wait_ge(w_lo, 3)
            dve.wait_ge(consts, 9)
            link(v.tensor_tensor(L, S[:, 3].rearrange("p (t e) -> p t e", t=NT), bc(bgr[:], sh3, 1), ALU.add))
            link(v.tensor_scalar(rev, iot[:, 0:NE], -1.0, float(NE), ALU.mult, ALU.add))
            link(v.tensor_scalar(j128, iot[:, 0:NT], float(P), None, ALU.mult))
            dve.wait_ge(g_done, 1)
            link(v.tensor_copy(iotf[:], iot[0:1, :]))
            src = L
            for c, oh in enumerate((OH1, OH2)):
                link(v.tensor_reduce(mk[:, 2 * c], src, AX.X, ALU.max))
                link(v.tensor_tensor(KEY, src, bc(mk[:, 2 * c], sh3, 2), ALU.is_equal))
                link(v.tensor_tensor(KEY, KEY, bc(rev, sh3, 1), ALU.mult))
                link(v.tensor_reduce(mk[:, 2 * c + 1], KEY, AX.X, ALU.max))
                link(v.tensor_tensor(oh, KEY, bc(mk[:, 2 * c + 1], sh3, 2), ALU.is_equal))
                if c == 0:
                    link(v.scalar_tensor_tensor(out=A, in0=OH1, scalar=-BIG, in1=L, op0=ALU.mult, op1=ALU.add))
                    src = A
            v.tensor_tensor(mk[:, 4], mk[:, 2], mk[:, 0], ALU.subtract).then_inc(dlt, 1)
            v.tensor_tensor(th[:].bitcast(BF16)[:, 0:NT * NE].rearrange("p (t e) -> p t e", t=NT), OH1, OH2,
                            ALU.add).then_inc(oh_ready, 1)
            link(v.memset(MASK, 1.0))
            MASKE = MASK.rearrange("p t e -> p (t e)")
            link(v.memset(MASKE.rearrange("p (e t) -> p e t", e=NE)[:, :, 0:1], 0.0))
            dve.wait_ge(exp_dlt, 1)
            link(v.tensor_scalar(mk[:, 6], mk[:, 5], 1.0, None, ALU.add))
            link(v.reciprocal(w12[:, 0], mk[:, 6]))
            link(v.tensor_tensor(w12[:, 1], w12[:, 0], mk[:, 5], ALU.mult))
            dve.wait_ge(rank_done, 1)
            flat = [P, NE, NT]
            TOT, INC = B_.rearrange("p t e -> p (t e)"), C.rearrange("p t e -> p (t e)")
            TOTE, INCE = TOT.rearrange("p (e t) -> p e t", e=NE), INC.rearrange("p (e t) -> p e t", e=NE)
            link(v.tensor_copy(TOTE, S[:, 1].rearrange("p (t e) -> p e t", t=NT)))
            link(v.tensor_tensor_scan(INC, MASKE, TOT, 0.0, ALU.mult, ALU.add))
            link(v.tensor_copy(small[:, 0], INCE[:, :, NT - 1]))
            KE = KEY.rearrange("p t e -> p (t e)").rearrange("p (e t) -> p e t", e=NE)
            link(v.tensor_tensor(KE, bc(small[:, 0], flat, 2), bc(j128, flat, 1), ALU.is_gt))
            link(v.tensor_reduce(small[:, 1], KE, AX.X, ALU.add))
            link(v.memset(small[:, 2], 1.0))
            link(v.tensor_tensor_scan(small[:, 3], small[:, 2], small[:, 1], 0.0, ALU.mult, ALU.add))
            link(v.tensor_tensor(small[:, 4], small[:, 3], small[:, 1], ALU.subtract))
            link(v.tensor_scalar(small[:, 5], small[:, 4], float(P), None, ALU.mult))
            link(v.tensor_tensor(INCE, INCE, TOTE, ALU.subtract))
            link(v.tensor_tensor(INCE, INCE, bc(small[:, 5], flat, 2), ALU.add))
            link(v.tensor_tensor(A, S[:, 0].rearrange("p (t e) -> p t e", t=NT), INCE.rearrange("p e t -> p t e"), ALU.add))
            for c, oh in enumerate((OH1, OH2)):
                link(v.tensor_tensor(KEY, oh, A, ALU.mult))
                link(v.tensor_reduce(mk[:, 6], KEY, AX.X, ALU.add))
                link(v.tensor_copy(posu[:, c], mk[:, 6]))
            link(v.tensor_scalar(eidf[:], iotf[:], small[0:1, 3, 0:1], None, ALU.is_ge))
            for e in range(1, NE - 1):
                link(v.scalar_tensor_tensor(out=eidf[:], in0=iotf[:], scalar=small[0:1, 3, e:e + 1], in1=eidf[:],
                                            op0=ALU.is_ge, op1=ALU.add))
            v.tensor_copy(eid[:], eidf[:]).then_inc(routed, 1)

            def energy_lo(m):
                dve.wait_ge(m_hi, m + 1)
                v.scalar_tensor_tensor(out=eTl[:], in0=M[:, 0:2 * P], scalar=SCALE, in1=eTh[:].bitcast(F32),
                                       op0=ALU.mult, op1=ALU.subtract).then_inc(m_lo, 1)

            def maxima(q, half):
                for j in range(4):
                    dve.wait_ge(score_done, 4 * q + j + 1)
                    ins = v.tensor_reduce(mx4[:, half, j:j + 1], S[:, j], AX.X, ALU.max)
                ins.then_inc(max4, 1)
                dve.wait_ge(max4, q + 1)
                v.tensor_reduce(nmax[:, half:half + 1], mx4[:, half], AX.X, ALU.max, negate=True).then_inc(max_ready, 1)

            def probs_lo(n, half):
                for j in range(4):
                    cols = slice(half * P, (half + 1) * P)
                    lo(n + j, j % 2, pTl[:, 4 * j:4 * j + 4, cols], pTh[:, 4 * j:4 * j + 4, cols])

            def combine(g, q):
                dve.wait_ge(exp_done, 4 * q + 8)
                v.tensor_reduce(den[:], dn[:, bass.ds(q, 2)], AX.X, ALU.add).then_inc(den_ready, 1)
                dve.wait_ge(den_ready, 2 * g + 1)
                v.reciprocal(rden[:], den[:]).then_inc(den_ready, 1)
                dve.wait_ge(den_ready, 2 * g + 2)
                dve.wait_ge(back_done, g + 1)
                dve.wait_ge(sg_ready, g + 1)
                for a in range(2):
                    ins = v.scalar_tensor_tensor(out=sg[:, a], in0=O[:, (2 + a) * P:(3 + a) * P], scalar=rden[:, a:a + 1],
                                                 in1=sg[:, a], op0=ALU.mult, op1=ALU.add)
                ins.then_inc(pre_ready, 1)

            def add_experts(dst, side, t, k, half_base, done):
                for c in range(2):
                    for a in range(2):
                        ins = v.scalar_tensor_tensor(out=dst[:, a], in0=xy[:, side, 2 * a + c],
                                                     scalar=w12[:, c, bass.ds(t + a, 1)], in1=dst[:, a],
                                                     op0=ALU.mult, op1=ALU.add)
                    if c == 0:
                        ins.then_inc(ffn_half, 1)
                        dve.wait_ge(ffn_half, 2 * k + half_base + 1)
                ins.then_inc(done, 1)

            def base(b, i):
                if b == 0:
                    return
                dve.wait_ge(rb_in, 16 * (i + 1))
                dve.wait_ge(gat_a, 64 * (i + 1))
                add_experts(rb, 0, 2 * i, i, 0, rb_ready)
                dve.wait_ge(xb_in, 16 * (i + 1) + 16 * NP)
                dve.wait_ge(gat_b, 64 * (i + 1))
                add_experts(xb, 1, 2 * i + TB, i, 1, base_ready)

            def attention(b):
                q0, g0, n0, m0 = b * TB, b * NP, T_ATT[b], M_ATT[b]
                energy_lo(m0)
                maxima(q0, 0)
                maxima(q0 + 1, 1)
                with dve.Fori(0, NP - 1) as i:
                    energy_lo(m0 + i + 1)
                    probs_lo(n0 + 8 * i, 0)
                    maxima(q0 + 2 * i + 2, 0)
                    probs_lo(n0 + 8 * i + 4, 1)
                    base(b, i)
                    maxima(q0 + 2 * i + 3, 1)
                    combine(g0 + i, q0 + 2 * i)
                i = NP - 1
                probs_lo(n0 + 8 * i, 0)
                probs_lo(n0 + 8 * i + 4, 1)
                base(b, i)
                combine(g0 + i, q0 + 2 * i)

            attention(0)

            def gate_up(g, u):
                dve.wait_ge(gu_done, g + 1)
                t3 = S[:, 2 * u:2 * u + 2].rearrange("p b (a s f) -> p (b a) s f", a=2, s=2)
                gate, up = (gu_sb[:, u, s].rearrange("p (a f) -> p a f", a=4) for s in range(2))
                v.tensor_scalar(gate, t3[:, :, 0], LIMIT, None, ALU.min).then_inc(gate_ready, 1)
                v.tensor_scalar(up, t3[:, :, 1], 1.0 - LIMIT, 1.0 + LIMIT, ALU.max, ALU.min).then_inc(up_ready, 1)
                dve.wait_ge(up_ready, g + 1)
                dve.wait_ge(gate_ready, g + 1)
                v.tensor_tensor(up, up, gate, ALU.mult).then_inc(au_ready, 1)

            def gated(g, u):
                dve.wait_ge(th_ready, g + 1)
                dve.wait_ge(au_ready, g + 1)
                v.scalar_tensor_tensor(out=gu_sb[:, u, 1], in0=th[:], scalar=1.0, in1=gu_sb[:, u, 1],
                                       op0=ALU.add, op1=ALU.mult).then_inc(ga_ready, 1)

            lo(T_MOE, 0, xTl[:], xTh[:])
            gate_up(0, 0)
            gated(0, 0)
            lo(T_MOE + 1, 1, xTl[:], xTh[:])

            def expert_step(g, vv, last=False):
                u = (vv + 1) % 2
                n = T_MOE + 2 * g
                gate_up(g, u)
                lo(n, 0, gTl[:], gTh[:])
                if not last:
                    lo(n + 1, 1, xTl[:], xTh[:])
                gated(g, u)

            with dve.Fori(0, NG // 2 - 1) as j:
                expert_step(2 * j + 1, 0)
                expert_step(2 * j + 2, 1)
            expert_step(NG - 1, 0, last=True)
            lo(T_MOE + 2 * NG - 1, 1, gTl[:], gTh[:])

            for c in range(CB):
                lo(T_PRO[1] + c, c % 2, bufs[c % 2][1][:], bufs[c % 2][0][:])
                spin_lo(1, c)
            dve.wait_ge(back_done, NP)
            dve.wait_ge(tanh_ready, NP)
            mean_step(1)
            for c in range(CB):
                lo(T_PRO[1] + CB + c, c % 2, sl[:, 4 * c:4 * c + 4], sh[:, 4 * c:4 * c + 4])
            attention(1)


_INS = ["L0_attn_x", "L0_attn_W_spin", "L0_attn_b_spin", "L0_attn_W_global", "L0_attn_W_J", "L0_attn_beta",
        "L0_ffn_Wg", "L0_ffn_bg", "L0_ffn_Wgu", "L0_ffn_bgu", "L0_ffn_Wd", "L0_ffn_bd"]


def kernel(**inputs):
    import numpy as _np
    import concourse.bacc as _bacc
    from concourse import mybir as _mybir
    from concourse.bass_utils import run_bass_kernel_spmd as _run

    nc = _bacc.Bacc("TRN2", target_bir_lowering=False, num_devices=1)
    arrays, args = {}, []
    for name in _INS:
        a = _np.ascontiguousarray(inputs[name])
        arrays[f"in_{name}"] = a
        args.append(nc.dram_tensor(f"in_{name}", a.shape, _mybir.dt.from_np(a.dtype), kind="ExternalInput").ap())
    shape = inputs["L0_attn_x"].shape
    args.append(nc.dram_tensor("out_y", shape, _mybir.dt.float32, kind="ExternalOutput").ap())
    build(nc, *args)
    r = _run(nc, [arrays], core_ids=[0])
    return r.results[0]["out_y"]
```

```python
from contextlib import ExitStack

import concourse.bass as bass
from concourse import mybir

F32 = mybir.dt.float32
F32R = mybir.dt.float32r
BF16 = mybir.dt.bfloat16
U32 = mybir.dt.uint32
I32 = mybir.dt.int32
ALU = mybir.AluOpType
ACT = mybir.ActivationFunctionType
AX = mybir.AxisListType

P = 128
EPS = 1e-5
LIMIT = 7.0
ALPHA = 1.702


def build(nc, x, W_spin, b_spin, W_global, W_J, beta, Wg, bg, Wgu, bgu, Wd, bd, out):
    NB, N, D = x.shape
    NE, _, F2 = Wgu.shape
    F = F2 // 2
    assert D == P and F == P and N % 512 == 0
    TB = N // P
    NT = NB * TB
    CB = TB // 4
    NCH = NT // 4
    NP = TB // 2
    NSLOT_TILES = 2 * NT + NE
    NG = NSLOT_TILES // 4
    WC = F2 + D
    SCALE = 1.0 / float(D) ** 0.5
    BIG = 3.0e38
    ROUTED_BY = 3
    SCATTER_STEP = 6
    assert NSLOT_TILES % 8 == 0 and NB == 2 and NE * NT == 512

    x_v = x.rearrange("b (p t) d -> b p t d", p=P)
    out_v = out.rearrange("b (p t) d -> b p t d", p=P)
    slots_x = nc.dram_tensor("slots_x", [NSLOT_TILES * P, D], F32, kind="Internal").ap()
    slots_y = nc.dram_tensor("slots_y", [NSLOT_TILES * P, D], F32, kind="Internal").ap()
    part = nc.dram_tensor("part", [P, TB, D], F32, kind="Internal").ap()
    bias_parts = nc.dram_tensor("bias_parts", [2, NE, WC], F32, kind="Internal").ap()
    slots_x_v = slots_x.rearrange("(s p) d -> p s d", p=P)
    slots_y_v = slots_y.rearrange("(s p) d -> p s d", p=P)

    with ExitStack() as ctx:
        def sb(name, shape, dt=F32):
            return ctx.enter_context(nc.sbuf_tensor(name, shape, dt))

        def ps(name, shape):
            return ctx.enter_context(nc.psum_tensor(name, shape, F32))

        def sem(name):
            return ctx.enter_context(nc.semaphore(name))

        xn = sb("xn", [P, NT, D])
        sTh, sTl = sb("sTh", [P, N], F32R), sb("sTl", [P, N], F32R)
        sh, sl = sb("sh", [P, TB, D], F32R), sb("sl", [P, TB, D], F32R)
        prob = sb("prob", [P, 2, N])
        pTh, pTl = sb("pTh", [P, TB, 2 * P], F32R), sb("pTl", [P, TB, 2 * P], F32R)
        wh, wl = sb("wh", [P, NE, WC], F32R), sb("wl", [P, NE, WC], F32R)
        wb = sb("wb", [P, NE, WC], F32R)
        eTh, eTl = sb("eTh", [P, 2 * P], F32R), sb("eTl", [P, 2 * P], F32R)
        oT = sb("oT", [P, 2 * P])
        gu_sb = sb("gu_sb", [P, 2, 2, 512])
        th = sb("th", [P, 512])
        xy = sb("xy", [P, 4, 4, D])
        sg = sb("sg", [P, 2, D])
        xb = sb("xb", [P, 2, D])
        rb = sb("rb", [P, 2, D])
        ident = sb("ident", [P, P])
        identr = sb("identr", [P, P], F32R)
        onesr = sb("onesr", [P, P], F32R)
        tri = sb("tri", [P, P], BF16)
        onesb = sb("onesb", [P, P], BF16)
        wspTh, wspTl = sb("wspTh", [P, P], F32R), sb("wspTl", [P, P], F32R)
        wjTh, wjTl = sb("wjTh", [P, P], F32R), sb("wjTl", [P, P], F32R)
        wglT = sb("wglT", [P, P])
        wgT2 = sb("wgT2", [P, 2 * NE], F32R)
        wgTh, wgTl = wgT2[:, 0:NE], wgT2[:, NE:2 * NE]
        gb = sb("gb", [P, D])
        bspin = sb("bspin", [P, 1])
        betac = sb("betac", [P, 1])
        bgr = sb("bgr", [P, NE])
        stats = sb("stats", [P, NT, 6])
        mv = sb("mv", [P, NT, 2])
        rstd = sb("rstd", [P, NT])
        shift = sb("shift", [P, NT])
        epsc = sb("epsc", [P, 1])
        msum = sb("msum", [P, CB + 1])
        mx4 = sb("mx4", [P, 2, 4])
        nmax = sb("nmax", [P, 2])
        dn = sb("dn", [P, NT, 4])
        den = sb("den", [P, 2])
        rden = sb("rden", [P, 2])
        iot = sb("iot", [P, NSLOT_TILES], I32)
        w12 = sb("w12", [P, 2, NT])
        posu = sb("posu", [P, 2, NT], U32)
        ends = sb("ends", [P, NE])
        count_of = sb("count_of", [1, NSLOT_TILES])
        eid = sb("eid", [1, NSLOT_TILES], I32)
        pTh_flat, pTl_flat = (w[:].rearrange("p a b -> p (a b)") for w in (pTh, pTl))

        def part_slot(k):
            return tuple(w[:, 512 * k:512 * k + 512].rearrange("p (a b) -> p a b", a=4) for w in (pTh_flat, pTl_flat))

        xT = [part_slot(k) for k in range(4)]
        gT = [part_slot(2), part_slot(3)]
        b_hl = tuple(w[0:NE, 2048:2048 + WC] for w in (pTh_flat, pTl_flat))
        xb_last = gu_sb[:, 0, 0].rearrange("p (a d) -> p a d", a=4)[:, 0:2]
        rb_last = gu_sb[:, 0, 0].rearrange("p (a d) -> p a d", a=4)[:, 2:4]
        mk = rb[:].rearrange("p a b -> p (a b)").rearrange("p (k t) -> p k t", t=NT)
        bufs = [gu_sb[:, a, c] for a in range(2) for c in range(2)]
        bufs += [xy[:, a].rearrange("p b d -> p (b d)") for a in range(4)]
        LOGIT, KEY, OH1, OH2, TOT, INC = (w.rearrange("p (t e) -> p t e", t=NT) for w in bufs[0:6])
        MASK = bufs[6].rearrange("p (e t) -> p e t", e=NE)
        small = bufs[7][:, 0:6 * NE].rearrange("p (k e) -> p k e", e=NE)
        rev, j128 = bufs[7][:, 6 * NE:7 * NE], bufs[7][:, 7 * NE:7 * NE + NT]
        w4_st = gu_sb[:, 0].rearrange("p a n -> p (a n)")[:, 0:4 * P].rearrange("p (a n) -> p a n", a=4)
        b_st = gu_sb[0:NE, 1].rearrange("p a n -> p (a n)")[:, 0:WC]
        b_ad = th[0:NE, 0:WC]

        S = ps("S", [P, 4, 512])
        T = ps("T", [P, 2, 512])
        O = ps("O", [P, 512])
        M = ps("M", [P, 512])

        def spin_bank(c):
            return (M[:], S[:, 0], S[:, 1], O[:])[c]

        def row_bank(c):
            return (S[:, 0], S[:, 1], O[:], M[:])[c]

        ld_x = [sem(f"ld_x{c}") for c in range(NCH)]
        ld_w, ld_b = sem("ld_w"), sem("ld_b")
        ld_gu, ld_d = sem("ld_gu"), sem("ld_d")
        consts = sem("consts")
        route_consts = sem("route_consts")
        zeroed = sem("zeroed")
        dchain = sem("dchain")
        rstd_in, rstd_mid = sem("rstd_in"), sem("rstd_mid")
        rstd_ready = sem("rstd_ready")
        xn_ready = [sem("xn_ready0"), sem("xn_ready1")]
        wt_turned, wt_hi, wt_done = sem("wt_turned"), sem("wt_hi"), sem("wt_done")
        t_fill, t_hi, t_lo = sem("t_fill"), sem("t_hi"), sem("t_lo")
        m_fill, m_hi, m_lo = sem("m_fill"), sem("m_hi"), sem("m_lo")
        xT_used = sem("xT_used")
        log_done = sem("log_done")
        mean_ready, g_done, g_ready = sem("mean_ready"), sem("g_done"), sem("g_ready")
        dlt, exp_dlt = sem("dlt"), sem("exp_dlt")
        eid_ready = sem("eid_ready")
        log_out = sem("log_out")
        oh_ready, rank_fill, rank_out, routed = sem("oh_ready"), sem("rank_fill"), sem("rank_out"), sem("routed")
        w_hi, w_lo = sem("w_hi"), sem("w_lo")
        b_adj, b_hi, b_lo = sem("b_adj"), sem("b_hi"), sem("b_lo")
        wb_clear, b_out, b_in = sem("wb_clear"), sem("b_out"), sem("b_in")
        score_done = sem("score_done")
        max4 = sem("max4")
        max_ready = sem("max_ready")
        exp_done = sem("exp_done")
        r_fill, r_hi, r_lo = sem("r_fill"), sem("r_hi"), sem("r_lo")
        e_fill, e_hi, e_lo = sem("e_fill"), sem("e_hi"), sem("e_lo")
        pv_done, oT_ready, back_done = sem("pv_done"), sem("oT_ready"), sem("back_done")
        den_ready, pre_ready, tanh_ready = sem("den_ready"), sem("pre_ready"), sem("tanh_ready")
        sg_half, sg_ready = sem("sg_half"), sem("sg_ready")
        xb_in, xb_out, base_ready, fin_ready = sem("xb_in"), sem("xb_out"), sem("base_ready"), sem("fin_ready")
        rb_in, rb_out, rb_ready = sem("rb_in"), sem("rb_out"), sem("rb_ready")
        gat_last = sem("gat_last")
        last_in = sem("last_in")
        scat = sem("scat")
        gat_a, gat_b = sem("gat_a"), sem("gat_b")
        ffn_half = sem("ffn_half")
        xg_in = [sem("xg_in0"), sem("xg_in1")]
        y_out = [sem("y_out0"), sem("y_out1")]
        gu_done, gate_ready, up_ready, au_ready = sem("gu_done"), sem("gate_ready"), sem("up_ready"), sem("au_ready")
        th_ready, ga_ready, y_done, y_ready = sem("th_ready"), sem("ga_ready"), sem("y_done"), sem("y_ready")

        T_PRO = [0, 0]
        n = NCH
        T_ATT = [n, 0]
        n += 4 * TB
        T_PRO[1] = n
        n += CB
        T_MOE = n
        n += 2 * NG
        T_ATT[1] = n
        M_PRO = [0, CB]

        def rows_fill(g):
            return T_MOE + (g if isinstance(g, int) and g < 2 else 2 * g - 2)

        def gated_fill(g):
            if isinstance(g, int) and g >= NG - 2:
                return T_MOE + g + NG
            return T_MOE + 2 * g + 3

        def bc(ap, shape, at):
            return ap.unsqueeze(at).broadcast_to(shape)

        block = ctx.enter_context(nc.Block())

        @block.sync
        def _(sp):
            with nc.allow_non_contiguous_dma(reason="small vectors"):
                def load_x(c):
                    b, t = c // CB, 4 * (c % CB)
                    sp.dma_start(xn[:, 4 * c:4 * c + 4], x_v[b][:, t:t + 4]).then_inc(ld_x[c], 16)

                load_x(0)
                load_x(1)
                sp.dma_start(w4_st[:, 0], W_spin).then_inc(ld_w, 16)
                sp.dma_start(w4_st[:, 1], W_J).then_inc(ld_w, 16)
                sp.dma_start(w4_st[:, 2], W_global).then_inc(ld_w, 16)
                sp.dma_start(w4_st[0:NE, 3], Wg).then_inc(ld_w, 16)
                sp.dma_start(bspin[:], b_spin.unsqueeze(1)).then_inc(ld_w, 16)
                sp.dma_start(betac[:], beta.partition_broadcast(P)).then_inc(ld_w, 16)
                sp.dma_start(bgr[:], bg.partition_broadcast(P)).then_inc(ld_w, 16)
                load_x(2)
                load_x(3)
                sp.dma_start(b_st[:, 0:F2], bgu).then_inc(ld_b, 16)
                sp.dma_start(b_st[:, F2:WC], bd).then_inc(ld_b, 16)
                for c in range(CB, NCH):
                    load_x(c)
                sp.dma_start(wl[:, :, F2:WC].bitcast(F32), Wd.rearrange("e k n -> k e n")).then_inc(ld_d, 16)
                sp.dma_start(wl[:, :, 0:F2].bitcast(F32), Wgu.rearrange("e k n -> k e n")).then_inc(ld_gu, 16)
                sp.wait_ge(consts, 2)
                sp.dma_start(
                    slots_x.rearrange("(p r) d -> p (r d)", p=P).rearrange("p (a n) -> p a n", n=2 * D),
                    bc(xb[:].rearrange("p a d -> p (a d)"), [P, NSLOT_TILES // 2, 2 * D], 1)).then_inc(zeroed, 16)
                sp.wait_ge(b_hi, 1)
                sp.dma_start(bias_parts[0], b_hl[0].bitcast(F32)).then_inc(b_out, 16)
                sp.wait_ge(b_lo, 1)
                sp.dma_start(bias_parts[1], b_hl[1].bitcast(F32)).then_inc(b_out, 16)
                sp.wait_ge(b_out, 32)
                sp.wait_ge(wb_clear, 1)
                sp.dma_start(wb[0:2].bitcast(F32), bias_parts).then_inc(b_in, 16)
                sp.wait_ge(zeroed, 16)
                for k in range(NP):
                    if k:
                        sp.wait_ge(xb_out, k * 16)
                    sp.dma_start(xb[:], x_v[0][:, 2 * k:2 * k + 2]).then_inc(xb_in, 16)
                    sp.wait_ge(fin_ready, k + 1)
                    sp.dma_start(part[:, 2 * k:2 * k + 2], xb[:]).then_inc(xb_out, 16)
                sp.wait_ge(scat, 16 * 2 * NT)
                for u in range(2):
                    sp.dma_start(xy[:, u], slots_x_v[:, 4 * u:4 * u + 4]).then_inc(xg_in[u], 16)

                for g in range(NG + 2):
                    if g + 2 < NG:
                        sp.wait_ge(t_fill, rows_fill(g) + 1)
                        sp.dma_start(xy[:, g % 2], slots_x_v[:, 4 * g + 8:4 * g + 12]).then_inc(xg_in[g % 2], 16)
                    if g >= 2:
                        sp.wait_ge(y_ready, g - 1)
                        sp.dma_start(slots_y_v[:, 4 * g - 8:4 * g - 4], xy[:, 2 + g % 2]).then_inc(y_out[g % 2], 16)
                sp.wait_ge(y_ready, NG)
                sp.dma_start(xb_last, x_v[1][:, TB - 2:TB]).then_inc(last_in, 16)
                sp.wait_ge(xb_out, NP * 16)
                sp.dma_start(rb_last, part[:, TB - 2:TB]).then_inc(last_in, 16)
                for k in range(NP):
                    last = k == NP - 1
                    if not last:
                        sp.wait_ge(xb_out, k * 16 + NP * 16)
                        sp.dma_start(xb[:], x_v[1][:, 2 * k:2 * k + 2]).then_inc(xb_in, 16)
                        if k:
                            sp.wait_ge(rb_out, k * 16)
                        sp.dma_start(rb[:], part[:, 2 * k:2 * k + 2]).then_inc(rb_in, 16)
                    sp.wait_ge(rb_ready, k + 1)
                    sp.dma_start(out_v[0][:, 2 * k:2 * k + 2], rb_last if last else rb[:]).then_inc(rb_out, 16)
                    sp.wait_ge(fin_ready, k + 1 + NP)
                    sp.dma_start(out_v[1][:, 2 * k:2 * k + 2], xb_last if last else xb[:]).then_inc(xb_out, 16)
                sp.wait_ge(xb_out, 2 * NP * 16)
                sp.wait_ge(rb_out, NP * 16)

        @block.gpsimd
        def _(pool):
            nc.gpsimd.memset(xb[:], 0.0).then_inc(consts, 1)
            nc.gpsimd.memset(ident[:], 0.0).then_inc(consts, 1)
            nc.gpsimd.memset(tri[:], 1.0).then_inc(consts, 1)
            nc.gpsimd.memset(onesb[:], 1.0).then_inc(consts, 1)
            nc.gpsimd.iota(iot[:], [[1, NSLOT_TILES]], base=0, channel_multiplier=0).then_inc(consts, 1)
            nc.gpsimd.memset(epsc[:], EPS).then_inc(consts, 1)
            nc.gpsimd.memset(onesr[:].bitcast(F32), 1.0).then_inc(consts, 1)
            pool.wait_ge(consts, 7)
            nc.gpsimd.affine_select(out=ident[:], in_=ident[:], compare_op=ALU.not_equal, fill=1.0, base=0,
                                    pattern=[[-1, P]], channel_multiplier=1).then_inc(consts, 1)
            nc.gpsimd.affine_select(out=tri[:], in_=tri[:], compare_op=ALU.is_gt, fill=0.0, base=0,
                                    pattern=[[1, P]], channel_multiplier=-1).then_inc(consts, 1)
            nc.gpsimd.memset(MASK, 1.0).then_inc(route_consts, 1)
            nc.gpsimd.tensor_scalar(rev, iot[:, 0:NE], -1.0, float(NE), ALU.mult, ALU.add).then_inc(route_consts, 1)
            nc.gpsimd.tensor_scalar(j128, iot[:, 0:NT], float(P), None, ALU.mult).then_inc(route_consts, 1)
            pool.wait_ge(route_consts, 1)
            nc.gpsimd.memset(MASK[:, :, 0:1], 0.0).then_inc(route_consts, 1)
            nc.gpsimd.memset(wb[:].bitcast(F32), 0.0).then_inc(wb_clear, 1)

            pool.wait_ge(ld_d, 16)
            pool.wait_ge(ld_gu, 16)

            def cut_weights(k):
                part = slice(k * NE // 4, (k + 1) * NE // 4)
                nc.gpsimd.tensor_copy(wh[:, part], wl[:, part].bitcast(F32)).then_inc(w_hi, 1)
                pool.wait_ge(w_hi, k + 1)
                nc.gpsimd.tensor_tensor(wl[:, part], wl[:, part].bitcast(F32), wh[:, part].bitcast(F32),
                                        ALU.subtract).then_inc(w_lo, 1)

            def fin(g):
                pool.wait_ge(tanh_ready, g + 1)
                if g < NP:
                    pool.wait_ge(xb_in, 16 * (g + 1))
                else:
                    pool.wait_ge(base_ready, g + 1 - NP)
                total = xb_last if g == 2 * NP - 1 else xb[:]
                nc.gpsimd.tensor_tensor(total, total, sg[:], ALU.add).then_inc(fin_ready, 1)

            def sg_step(g):
                k = g % NP
                if g:
                    pool.wait_ge(fin_ready, g)
                if k == 0:
                    pool.wait_ge(r_lo, (g // NP + 1) * CB)
                    pool.wait_ge(g_ready, g // NP + 1)
                nc.gpsimd.tensor_tensor(sg[:], sh[:, 2 * k:2 * k + 2].bitcast(F32), sl[:, 2 * k:2 * k + 2].bitcast(F32),
                                        ALU.add).then_inc(sg_half, 1)
                pool.wait_ge(sg_half, g + 1)
                nc.gpsimd.tensor_tensor(sg[:], sg[:], bc(gb[:], [P, 2, D], 1), ALU.add).then_inc(sg_ready, 1)

            def scatter(first, last):
                for t in range(first, last):
                    for c in range(2):
                        pool.indirect_dma_start(slots_x, bass.IndirectOffsetOnAxis(ap=posu[:, c, t:t + 1], axis=0),
                                                xn[:, t], None).then_inc(scat, 16)

            for k in range(NP):
                if k:
                    fin(k - 1)
                sg_step(k)
                if k == 0:
                    for part in range(4):
                        cut_weights(part)
                if k == ROUTED_BY:
                    pool.wait_ge(zeroed, 16)
                    pool.wait_ge(routed, 1)
                if k >= ROUTED_BY:
                    scatter(SCATTER_STEP * (k - ROUTED_BY), SCATTER_STEP * (k - ROUTED_BY + 1))
            fin(NP - 1)
            scatter(SCATTER_STEP * (NP - ROUTED_BY), NT)
            with pool.Fori(0, NG // 2) as j:
                for u in range(2):
                    pool.wait_ge(up_ready, 2 * j + u + 1)
                    pool.wait_ge(gate_ready, 2 * j + u + 1)
                    nc.gpsimd.tensor_tensor(gu_sb[:, u, 1], gu_sb[:, u, 1], gu_sb[:, u, 0], ALU.mult).then_inc(au_ready, 1)
            pool.wait_ge(y_out[0], 16 * (NG // 2))
            pool.wait_ge(y_out[1], 16 * (NG // 2))
            def gather(side, t, c, done):
                pool.indirect_dma_start(xy[:, side, 2 * (t % 2) + c], None, slots_y,
                                        bass.IndirectOffsetOnAxis(ap=posu[:, c, t:t + 1], axis=0)).then_inc(done, 16)

            for k in range(NP):
                if k:
                    fin(NP + k - 1)
                sg_step(NP + k)
                if k < NP - 1:
                    for side, (done, t0) in enumerate(((gat_a, 2 * k), (gat_b, TB + 2 * k))):
                        if k:
                            pool.wait_ge(rb_ready if side == 0 else base_ready, k)
                        for t in range(2):
                            for c in range(2):
                                gather(side, t0 + t, c, done)
                if NP - 5 <= k < NP - 1:
                    t = k - (NP - 5)
                    for c in range(2):
                        gather(2 + t // 2, (t // 2) * TB + TB - 2 + t % 2, c, gat_last)
            fin(2 * NP - 1)

        @block.tensor
        def _(pe):
            def three(o, ah, al, bh, bl, start=True, stop=True):
                nc.tensor.matmul(o, ah, bh, start=start, stop=False)
                nc.tensor.matmul(o, ah, bl, start=False, stop=False)
                return nc.tensor.matmul(o, al, bh, start=False, stop=stop)

            def t_free(n):
                if not isinstance(n, int) or n >= 2:
                    pe.wait_ge(t_lo, n - 1)

            def turn(n, tile, parity, ready=None):
                t_free(n)
                for a in range(4):
                    m = nc.tensor.transpose(T[:, parity, a * P:(a + 1) * P], tile(a), ident[:])
                m.then_inc(t_fill, 1)

            pe.wait_ge(consts, 9)
            pe.wait_ge(ld_w, 112)
            for a in range(3):
                nc.tensor.transpose(S[:, 0, a * P:(a + 1) * P], w4_st[:, a], ident[:])
            nc.tensor.transpose(S[:, 0, 3 * P:3 * P + NE], w4_st[0:NE, 3], ident[0:NE, 0:NE]).then_inc(wt_turned, 1)

            def spin(c):
                xh, xl = xT[c % 4]
                three(spin_bank(c), wspTh[:], wspTl[:], flat(xh), flat(xl)).then_inc(m_fill, 1)

            def flat(ap):
                return ap.rearrange("p a b -> p (a b)")

            def turn_tokens(b, c, n):
                pe.wait_ge(xn_ready[b], c + 1)
                turn(n, lambda a: xn[:, b * TB + 4 * c + a], n % 2)

            def energy(i):
                lo, hi = sTl[:, bass.ds(i * 2 * P, 2 * P)], sTh[:, bass.ds(i * 2 * P, 2 * P)]
                three(M[:, 0:2 * P], wjTh[:], wjTl[:], hi, lo).then_inc(e_fill, 1)

            def row_of_s(b, c):
                pe.wait_ge(m_lo, M_PRO[b] + CB)
                if c == 3:
                    pe.wait_ge(e_lo, b * NP + 1)
                for a in range(4):
                    o = row_bank(c)[:, a * P:(a + 1) * P]
                    nc.tensor.matmul(o, sTh[:, (4 * c + a) * P:(4 * c + a + 1) * P], identr[:], start=True, stop=False)
                    m = nc.tensor.matmul(o, sTl[:, (4 * c + a) * P:(4 * c + a + 1) * P], identr[:], start=False, stop=True)
                m.then_inc(r_fill, 1)

            turn_tokens(0, 0, 0)
            turn_tokens(0, 1, 1)
            pe.wait_ge(wt_done, 1)
            for c in range(NCH):
                pe.wait_ge(t_lo, c + 1)
                if c < CB:
                    spin(c)
                if c + 2 < NCH:
                    turn_tokens((c + 2) // CB, (c + 2) % CB, c + 2)
                if c == CB:
                    pe.wait_ge(m_lo, CB)
                    energy(0)
                if c >= CB:
                    row_of_s(0, c - CB)
                xh, xl = xT[c % 4]
                for a in range(4):
                    o = S[:, 2:4].rearrange("p b n -> p (b n)")[:, (4 * c + a) * 2 * NE:(4 * c + a + 1) * 2 * NE]
                    nc.tensor.matmul(o, xh[:, a], wgT2[:], start=True, stop=False)
                    m = nc.tensor.matmul(o[:, 0:NE], xl[:, a], wgT2[:, 0:NE], start=False, stop=True)
                m.then_inc(log_done, 1)

            def global_row(b):
                pe.wait_ge(r_lo, b * CB + 3)
                pe.wait_ge(mean_ready, b + 1)
                nc.tensor.matmul(O[:, 0:D], mean_bc, wglT[:], start=True, stop=True).then_inc(g_done, 1)

            mean_bc = oT[:, 0:P]
            ohb = th[:].bitcast(BF16)[:, 0:NT * NE]

            def count_pairs(k):
                if k == 0:
                    pe.wait_ge(oh_ready, 1)
                nc.tensor.matmul(M[:], (onesb, tri)[k][:], ohb, start=True, stop=True).then_inc(rank_fill, 1)

            def score(q, half, j):
                if not (isinstance(q, int) and q == 0):
                    pe.wait_ge(exp_done, 4 * q - 4 + j + 1)
                e_h, e_l = eTh[:, half * P:(half + 1) * P], eTl[:, half * P:(half + 1) * P]
                three(S[:, j], e_h, e_l, sTh[:, 512 * j:512 * j + 512],
                      sTl[:, 512 * j:512 * j + 512]).then_inc(score_done, 1)

            def turn_prob(q, half, n, j):
                t_free(n + j)
                pe.wait_ge(exp_done, 4 * q + j + 1)
                for a in range(4):
                    m = nc.tensor.transpose(T[:, j % 2, a * P:(a + 1) * P],
                                            prob[:, half, (4 * j + a) * P:(4 * j + a + 1) * P], ident[:])
                m.then_inc(t_fill, 1)

            def stage(q, half, n, first=0):
                for j in range(first, 4):
                    turn_prob(q, half, n, j)
                    score(q + 1, 1 - half, j)

            def values(n, first, last):
                for t in range(first, last):
                    if t % 4 == 0:
                        pe.wait_ge(t_lo, n + 4 + t // 4 + 1)
                    m = three(O[:, 0:2 * P], sh[:, t], sl[:, t], pTh[:, t], pTl[:, t], start=t == 0, stop=t == TB - 1)
                if last == TB:
                    m.then_inc(pv_done, 1)

            def turn_back(g):
                pe.wait_ge(oT_ready, g + 1)
                nc.tensor.transpose(O[:, 2 * P:3 * P], oT[:, 0:P], ident[:])
                nc.tensor.transpose(O[:, 3 * P:4 * P], oT[:, P:2 * P], ident[:]).then_inc(back_done, 1)

            def attention(b):
                q0, g0, n0 = b * TB, b * NP, T_ATT[b]
                if b == 0:
                    pe.wait_ge(e_lo, 1)
                    pe.wait_ge(r_lo, 2)
                    score(q0, 0, 0)
                    score(q0, 0, 1)
                    pe.wait_ge(log_out, 2)
                    score(q0, 0, 2)
                    score(q0, 0, 3)
                    global_row(0)
                stage(q0, 0, n0)
                pe.wait_ge(r_lo, (b + 1) * CB)
                energy(1)
                turn_prob(q0 + 1, 1, n0 + 4, 0)
                pe.wait_ge(e_lo, g0 + 2)
                score(q0 + 2, 0, 0)
                pe.wait_ge(g_ready, b + 1)

                def pair(i, last=False):
                    stage(q0 + 2 * i + 1, 1, n0 + 8 * i + 4, first=1)
                    if b == 0 and isinstance(i, int) and i == 2:
                        count_pairs(1)
                    values(n0 + 8 * i, 0, 8)
                    if b == 0 and isinstance(i, int) and i == 1:
                        count_pairs(0)
                    values(n0 + 8 * i, 8, TB - 4)
                    stage(q0 + 2 * i + 2, 0, n0 + 8 * i + 8)
                    if b == 0 and isinstance(i, int) and i in (1, 2):
                        pe.wait_ge(rank_out, i)
                    if not last:
                        energy(i + 2)
                    values(n0 + 8 * i, TB - 4, TB)
                    turn_prob(q0 + 2 * i + 3, 1, n0 + 8 * i + 12, 0)
                    if not last:
                        pe.wait_ge(e_lo, g0 + i + 3)
                        score(q0 + 2 * i + 4, 0, 0)
                    turn_back(g0 + i)

                straight = 3 if b == 0 else 0
                for i in range(straight):
                    pair(i)
                with pe.Fori(straight, NP - 2) as i:
                    pair(i)
                pair(NP - 2, last=True)
                i = NP - 1
                for j in range(1, 4):
                    turn_prob(q0 + 2 * i + 1, 1, n0 + 8 * i + 4, j)
                values(n0 + 8 * i, 0, TB)
                turn_back(g0 + i)

            attention(0)

            pe.wait_ge(exp_done, 4 * TB)
            pe.wait_ge(pre_ready, NP)
            turn_tokens(1, 0, T_PRO[1])
            turn_tokens(1, 1, T_PRO[1] + 1)
            for c in range(CB):
                pe.wait_ge(t_lo, T_PRO[1] + c + 1)
                spin(c)
                if c + 2 < CB:
                    turn_tokens(1, c + 2, T_PRO[1] + c + 2)
            pe.wait_ge(m_lo, 2 * CB)
            energy(0)
            for c in range(CB):
                row_of_s(1, c)
            global_row(1)
            pe.wait_ge(r_lo, 2 * CB)

            wh2, wl2, wb2 = (w[:].rearrange("p e n -> p (e n)") for w in (wh, wl, wb))

            def experts_of(g):
                _, columns = nc.values_load_multi_w_load_instructions(
                    eid[0:1, bass.ds(4 * g, 4)], engines=(mybir.EngineType.PE,), min_val=0, max_val=(NE - 1) * WC,
                    skip_runtime_bounds_check_because="the chip's own list of experts")
                return columns

            def turn_slots(g, u, bank, count):
                pe.wait_ge(xg_in[u], count)
                for a in range(4):
                    m = nc.tensor.transpose(T[:, bank, a * P:(a + 1) * P], xy[:, u, a], ident[:])
                m.then_inc(t_fill, 1)

            def gate_up(g, u):
                xh, xl = xT[u]
                for a, e in enumerate(experts_of(g)):
                    o = S[:, 2 * u + a // 2, (a % 2) * F2:(a % 2 + 1) * F2]
                    cols = bass.ds(e, F2)
                    nc.tensor.matmul(o, onesr[:], wb2[:, cols], start=True, stop=False)
                    m = three(o, xh[:, a], xl[:, a], wh2[:, cols], wl2[:, cols], start=False)
                m.then_inc(gu_done, 1)

            def turn_gated(g, u, bank):
                pe.wait_ge(ga_ready, g + 1)
                for a in range(4):
                    m = nc.tensor.transpose(T[:, bank, a * P:(a + 1) * P], gu_sb[:, u, 1, a * P:(a + 1) * P], ident[:])
                m.then_inc(t_fill, 1)

            def down(g, u):
                gh, gl = gT[u]
                for a, e in enumerate(experts_of(g)):
                    cols = bass.ds(e + F2, D)
                    o = (O, M)[u][:, a * P:(a + 1) * P]
                    nc.tensor.matmul(o, onesr[:], wb2[:, cols], start=True, stop=False)
                    m = three(o, gh[:, a], gl[:, a], wh2[:, cols], wl2[:, cols], start=False)
                m.then_inc(y_done, 1)

            def expert_step(g, u, count, rows=True, results=True):
                pe.wait_ge(t_lo, rows_fill(g) + 1)
                if rows:
                    turn_slots(g + 1, 1 - u, 0, count)
                gate_up(g, u)
                turn_gated(g - 1, 1 - u, 1 if rows else 0)
                if results:
                    down(g - 2, u)

            pe.wait_ge(w_lo, 4)
            pe.wait_ge(b_in, 16)
            pe.wait_ge(eid_ready, 1)
            pe.wait_ge(g_ready, 2)
            pe.wait_ge(t_lo, T_MOE)
            turn_slots(0, 0, 0, 16)
            turn_slots(1, 1, 1, 16)
            pe.wait_ge(t_lo, rows_fill(0) + 1)
            gate_up(0, 0)
            expert_step(1, 1, 32, results=False)
            expert_step(2, 0, 32)
            expert_step(3, 1, 48)
            with pe.Fori(2, NG // 2 - 1) as j:
                expert_step(2 * j, 0, 16 * (j + 1))
                expert_step(2 * j + 1, 1, 16 * (j + 2))
            expert_step(NG - 2, 0, 16 * (NG // 2))
            expert_step(NG - 1, 1, 0, rows=False)
            pe.wait_ge(up_ready, NG - 1)
            score(TB, 0, 0)
            score(TB, 0, 1)
            pe.wait_ge(t_lo, gated_fill(NG - 2) + 1)
            down(NG - 2, 0)
            turn_gated(NG - 1, 1, 1)
            pe.wait_ge(up_ready, NG)
            score(TB, 0, 2)
            score(TB, 0, 3)
            pe.wait_ge(t_lo, gated_fill(NG - 1) + 1)
            down(NG - 1, 1)

            pe.wait_ge(y_ready, NG)
            attention(1)

        @block.scalar
        def _(act):
            def hi(n, parity, dst, src=None):
                act.wait_ge(t_fill, n + 1)
                nc.scalar.activation(dst, T[:, parity].rearrange("p (a b) -> p a b", a=4), ACT.Copy).then_inc(t_hi, 1)

            act.wait_ge(consts, 9)
            nc.scalar.activation(identr[:], ident[:], ACT.Copy).then_inc(wt_hi, 1)

            def deviation(c):
                act.wait_ge(rstd_in, c + 1)
                nc.scalar.activation(rstd[:, 4 * c:4 * c + 4], mv[:, 4 * c:4 * c + 4, 1], ACT.Sqrt,
                                     bias=epsc[:]).then_inc(rstd_mid, 1)

            def normalise(c):
                act.wait_ge(rstd_ready, c + 1)
                for t in range(4 * c, 4 * c + 4):
                    ins = nc.scalar.activation(xn[:, t], xn[:, t], ACT.Identity, bias=shift[:, t:t + 1],
                                               scale=rstd[:, t:t + 1])
                ins.then_inc(xn_ready[0], 1)

            deviation(0)
            deviation(1)
            normalise(0)
            deviation(2)
            normalise(1)
            act.wait_ge(wt_turned, 1)
            nc.scalar.activation(wspTh[:], S[:, 0, 0:P], ACT.Copy).then_inc(wt_hi, 1)
            nc.scalar.activation(wjTh[:], S[:, 0, P:2 * P], ACT.Copy).then_inc(wt_hi, 1)
            nc.scalar.activation(wglT[:], S[:, 0, 2 * P:3 * P], ACT.Copy).then_inc(wt_hi, 1)
            nc.scalar.activation(wgTh, S[:, 0, 3 * P:3 * P + NE], ACT.Copy).then_inc(wt_hi, 1)

            def spin_hi(b, c):
                act.wait_ge(m_fill, M_PRO[b] + c + 1)
                nc.scalar.activation(sTh[:, 512 * c:512 * c + 512], spin_bank(c), ACT.Identity, bias=bspin[:],
                                     accum_out=msum[:, c:c + 1]).then_inc(m_hi, 1)

            def tokens_hi(c, n):
                if 4 <= n < NCH:
                    act.wait_ge(log_done, n - 3)
                hi(n, n % 2, xT[c % 4][0])

            def row_hi(b, c):
                act.wait_ge(r_fill, b * CB + c + 1)
                nc.scalar.activation(sh[:, 4 * c:4 * c + 4], row_bank(c).rearrange("p (a b) -> p a b", a=4),
                                     ACT.Copy).then_inc(r_hi, 1)

            def energy_hi(g):
                act.wait_ge(e_fill, g + 1)
                nc.scalar.activation(eTh[:], M[:, 0:2 * P], ACT.Copy, scale=SCALE).then_inc(e_hi, 1)

            tokens_hi(0, 0)
            deviation(3)
            normalise(2)
            tokens_hi(1, 1)
            normalise(3)
            for c in range(NCH):
                if c < CB:
                    spin_hi(0, c)
                if c < 2:
                    tokens_hi(c + 2, c + 2)
                if c < CB:
                    deviation(CB + c)
                if 2 <= c < NCH - 2:
                    tokens_hi(c + 2, c + 2)
                if c == CB:
                    energy_hi(0)
                if c >= CB:
                    row_hi(0, c - CB)
                if c == 1:
                    act.wait_ge(b_adj, 1)
                    nc.scalar.activation(b_hl[0], b_ad, ACT.Copy).then_inc(b_hi, 1)

            def expo(q, half, j):
                nc.scalar.activation(prob[:, half, 512 * j:512 * j + 512], S[:, j], ACT.Exp, bias=nmax[:, half:half + 1],
                                     accum_out=dn2[:, bass.ds(4 * q + j, 1)]).then_inc(exp_done, 1)

            def prob_hi(n, half, j):
                hi(n + j, j % 2, pTh[:, 4 * j:4 * j + 4, half * P:(half + 1) * P])

            def stage(q, half, n):
                for j in range(3):
                    expo(q, half, j + 1)
                    prob_hi(n, half, j)
                prob_hi(n, half, 3)

            dn2 = dn[:].rearrange("p t j -> p (t j)")

            def tanh_step(g):
                act.wait_ge(pre_ready, g + 1)
                nc.scalar.activation(sg[:], sg[:], ACT.Tanh, scale=betac[:]).then_inc(tanh_ready, 1)

            def attention(b):
                q0, g0, n0 = b * TB, b * NP, T_ATT[b]
                if b == 0:
                    act.wait_ge(log_done, NCH)
                    act.wait_ge(b_out, 32)
                if b == 0:
                    global_copy(0)
                act.wait_ge(max_ready, q0 + 1)
                expo(q0, 0, 0)
                stage(q0, 0, n0)
                energy_hi(g0 + 1)
                act.wait_ge(max_ready, q0 + 2)
                expo(q0 + 1, 1, 0)

                def pair(i, first=False, last=False):
                    stage(q0 + 2 * i + 1, 1, n0 + 8 * i + 4)
                    if not first:
                        tanh_step(g0 + i - 1)
                    act.wait_ge(max_ready, q0 + 2 * i + 3)
                    for j in range(4):
                        expo(q0 + 2 * i + 2, 0, j)
                    if b == 0 and isinstance(i, int) and i == 1:
                        act.wait_ge(dlt, 1)
                        nc.scalar.activation(mk[:, 5], mk[:, 4], ACT.Exp).then_inc(exp_dlt, 1)
                    for j in range(3):
                        prob_hi(n0 + 8 * i + 8, 0, j)
                    if not last:
                        energy_hi(g0 + i + 2)
                    act.wait_ge(max_ready, q0 + 2 * i + 4)
                    expo(q0 + 2 * i + 3, 1, 0)
                    act.wait_ge(pv_done, g0 + i + 1)
                    prob_hi(n0 + 8 * i + 8, 0, 3)

                straight = 2 if b == 0 else 1
                for i in range(straight):
                    pair(i, first=i == 0)
                with act.Fori(straight, NP - 2) as i:
                    pair(i)
                pair(NP - 2, last=True)
                i = NP - 1
                stage(q0 + 2 * i + 1, 1, n0 + 8 * i + 4)
                tanh_step(g0 + i - 1)
                tanh_step(g0 + i)

            def global_copy(b):
                act.wait_ge(g_done, b + 1)
                nc.scalar.activation(gb[:], O[:, 0:D], ACT.Copy).then_inc(g_ready, 1)

            attention(0)

            tokens_hi(0, T_PRO[1])
            tokens_hi(1, T_PRO[1] + 1)
            for c in range(CB):
                spin_hi(1, c)
                if c + 2 < CB:
                    tokens_hi(c + 2, T_PRO[1] + c + 2)
            energy_hi(NP)
            act.wait_ge(sg_ready, NP)
            for c in range(CB):
                row_hi(1, c)
            global_copy(1)

            def rows_hi(n, bank, g, u):
                if not (isinstance(g, int) and g < 2):
                    act.wait_ge(gu_done, g - 1)
                hi(n, bank, xT[u][0])

            def gated_hi(n, bank, g, u):
                if not (isinstance(g, int) and g < 2):
                    act.wait_ge(y_done, g - 1)
                hi(n, bank, gT[u][0])

            def sigmoid_half(g, u):
                act.wait_ge(gate_ready, g + 1)
                if not (isinstance(g, int) and g == 0):
                    act.wait_ge(ga_ready, g)
                nc.scalar.activation(th[:], gu_sb[:, u, 0], ACT.Tanh, scale=ALPHA).then_inc(th_ready, 1)

            def y_copy(g, u, stored):
                act.wait_ge(y_done, g + 1)
                if not (isinstance(stored, int) and stored == 0):
                    act.wait_ge(y_out[u], stored)
                nc.scalar.activation(xy[:, 2 + u], (O, M)[u][:].rearrange("p (a d) -> p a d", a=4),
                                     ACT.Copy).then_inc(y_ready, 1)

            rows_hi(T_MOE, 0, 0, 0)
            rows_hi(T_MOE + 1, 1, 1, 1)
            sigmoid_half(0, 0)

            def expert_step(g, u, stored, rows=True, results=True):
                if rows:
                    rows_hi(T_MOE + 2 * g, 0, g + 1, 1 - u)
                gated_hi(T_MOE + 2 * g + (1 if rows else 0), 1 if rows else 0, g - 1, 1 - u)
                sigmoid_half(g, u)
                if results:
                    y_copy(g - 2, u, stored)

            expert_step(1, 1, 0, results=False)
            expert_step(2, 0, 0)
            expert_step(3, 1, 0)
            with act.Fori(2, NG // 2 - 1) as j:
                expert_step(2 * j, 0, 16 * j - 16)
                expert_step(2 * j + 1, 1, 16 * j - 16)
            expert_step(NG - 2, 0, 16 * (NG // 2 - 2))
            expert_step(NG - 1, 1, 16 * (NG // 2 - 2), rows=False)
            y_copy(NG - 2, 0, 16 * (NG // 2 - 1))
            gated_hi(T_MOE + 2 * NG - 1, 1, NG - 1, 1)
            y_copy(NG - 1, 1, 16 * (NG // 2 - 1))

            attention(1)

        @block.vector
        def _(dve):
            v = nc.vector
            count = [0]

            def link(ins):
                count[0] += 1
                ins.then_inc(dchain, 1)
                dve.wait_ge(dchain, count[0])

            def lo(n, parity, dst, high):
                dve.wait_ge(t_hi, n + 1)
                v.tensor_tensor(dst, T[:, parity].rearrange("p (a b) -> p a b", a=4), high.bitcast(F32),
                                ALU.subtract).then_inc(t_lo, 1)

            def spin_lo(b, c):
                dve.wait_ge(m_hi, M_PRO[b] + c + 1)
                v.scalar_tensor_tensor(out=sTl[:, 512 * c:512 * c + 512], in0=spin_bank(c), scalar=bspin[:],
                                       in1=sTh[:, 512 * c:512 * c + 512].bitcast(F32), op0=ALU.add,
                                       op1=ALU.subtract).then_inc(m_lo, 1)

            def mean_step(b):
                dve.wait_ge(m_hi, M_PRO[b] + CB)
                link(v.tensor_reduce(msum[:, CB:CB + 1], msum[:, 0:CB], AX.X, ALU.add))
                link(v.tensor_scalar(msum[:, CB:CB + 1], msum[:, CB:CB + 1], 1.0 / N, None, ALU.mult))
                v.tensor_scalar(oT[:, 0:P], ident[:], 0.0, msum[:, CB:CB + 1], ALU.mult, ALU.add).then_inc(mean_ready, 1)

            def moments(c):
                dve.wait_ge(ld_x[c], 16)
                for t in range(4 * c, 4 * c + 4):
                    ins = v.bn_stats(stats[:, t], xn[:, t])
                link(ins)
                for t in range(4 * c, 4 * c + 4):
                    ins = v.bn_aggr(mv[:, t], stats[:, t])
                ins.then_inc(rstd_in, 1)

            def inverse(c):
                dve.wait_ge(rstd_mid, c + 1)
                r = rstd[:, 4 * c:4 * c + 4]
                link(v.reciprocal(r, r))
                v.scalar_tensor_tensor(out=shift[:, 4 * c:4 * c + 4], in0=mv[:, 4 * c:4 * c + 4, 0], scalar=-1.0, in1=r,
                                       op0=ALU.mult, op1=ALU.mult).then_inc(rstd_ready, 1)

            def normalise(c):
                dve.wait_ge(rstd_mid, c + 1)
                r = rstd[:, 4 * c:4 * c + 4]
                link(v.reciprocal(r, r))
                for t in range(4 * c, 4 * c + 4):
                    ins = v.tensor_scalar(xn[:, t], xn[:, t], mv[:, t, 0:1], rstd[:, t:t + 1], ALU.subtract, ALU.mult)
                ins.then_inc(xn_ready[1], 1)

            moments(0)
            moments(1)
            inverse(0)
            moments(2)
            inverse(1)
            moments(3)
            inverse(2)
            dve.wait_ge(wt_hi, 5)
            v.tensor_tensor(wspTl[:], S[:, 0, 0:P], wspTh[:].bitcast(F32), ALU.subtract)
            v.tensor_tensor(wjTl[:], S[:, 0, P:2 * P], wjTh[:].bitcast(F32), ALU.subtract)
            v.tensor_tensor(wgTl, S[:, 0, 3 * P:3 * P + NE], wgTh.bitcast(F32), ALU.subtract).then_inc(wt_done, 1)
            def tokens_lo(c, n):
                lo(n, n % 2, xT[c % 4][1], xT[c % 4][0])

            def row_lo(b, c):
                dve.wait_ge(r_hi, b * CB + c + 1)
                v.tensor_tensor(sl[:, 4 * c:4 * c + 4], row_bank(c).rearrange("p (a b) -> p a b", a=4),
                                sh[:, 4 * c:4 * c + 4].bitcast(F32), ALU.subtract).then_inc(r_lo, 1)

            def energy_lo(g):
                dve.wait_ge(e_hi, g + 1)
                v.scalar_tensor_tensor(out=eTl[:], in0=M[:, 0:2 * P], scalar=SCALE, in1=eTh[:].bitcast(F32),
                                       op0=ALU.mult, op1=ALU.subtract).then_inc(e_lo, 1)

            def of_batch(w, b):
                return w[:, b * TB:(b + 1) * TB]

            def copy_logits(b):
                dve.wait_ge(log_done, (b + 1) * CB)
                dve.wait_ge(ld_w, 112)
                parts = S[:, 2 + b].rearrange("p (t k e) -> p t k e", k=2, e=NE)
                L = of_batch(LOGIT, b)
                link(v.tensor_tensor(L, parts[:, :, 0], bc(bgr[:], [P, TB, NE], 1), ALU.add))
                v.tensor_tensor(L, L, parts[:, :, 1], ALU.add).then_inc(log_out, 1)

            def best(L, K, top, place):
                sh3 = list(L.shape)
                link(v.tensor_reduce(top, L, AX.X, ALU.max))
                link(v.tensor_tensor(K, L, bc(top, sh3, 2), ALU.is_equal))
                link(v.tensor_tensor(K, K, bc(rev, sh3, 1), ALU.mult))
                link(v.tensor_reduce(place, K, AX.X, ALU.max))

            def first_choice(b):
                dve.wait_ge(log_out, b + 1)
                dve.wait_ge(route_consts, 4)
                place = of_batch(mk[:, 1], b)
                best(of_batch(LOGIT, b), of_batch(KEY, b), of_batch(mk[:, 0], b), place)
                link(v.tensor_tensor(of_batch(OH1, b), of_batch(KEY, b), bc(place, [P, TB, NE], 2), ALU.is_equal))

            def second_choice():
                link(v.scalar_tensor_tensor(out=LOGIT, in0=OH1, scalar=-BIG, in1=LOGIT, op0=ALU.mult, op1=ALU.add))
                best(LOGIT, KEY, mk[:, 2], mk[:, 3])

            tokens_lo(0, 0)
            inverse(3)
            tokens_lo(1, 1)
            for c in range(NCH):
                if c < CB:
                    spin_lo(0, c)
                if c < 2:
                    tokens_lo(c + 2, c + 2)
                if c < CB:
                    moments(CB + c)
                if 1 <= c <= CB:
                    normalise(CB + c - 1)
                if 2 <= c < NCH - 2:
                    tokens_lo(c + 2, c + 2)
                if c == CB:
                    energy_lo(0)
                    mean_step(0)
                if c >= CB:
                    row_lo(0, c - CB)
                if c == CB + 1:
                    copy_logits(0)
                if c == CB + 3:
                    first_choice(0)
                if c == 0:
                    dve.wait_ge(ld_b, 32)
                    pairs = "p (f s) -> p f s"
                    v.tensor_copy(b_ad[:, F2:WC], b_st[:, F2:WC])
                    v.tensor_copy(b_ad[:, 0:F2].rearrange(pairs, s=2)[:, :, 0], b_st[:, 0:F2].rearrange(pairs, s=2)[:, :, 0])
                    v.tensor_scalar(b_ad[:, 0:F2].rearrange(pairs, s=2)[:, :, 1], b_st[:, 0:F2].rearrange(pairs, s=2)[:, :, 1],
                                    1.0, None, ALU.add).then_inc(b_adj, 1)
                if c == 2:
                    dve.wait_ge(b_hi, 1)
                    v.tensor_tensor(b_hl[1], b_ad, b_hl[0].bitcast(F32), ALU.subtract).then_inc(b_lo, 1)

            def choices():
                v.tensor_tensor(mk[:, 4], mk[:, 2], mk[:, 0], ALU.subtract).then_inc(dlt, 1)
                link(v.tensor_tensor(OH2, KEY, bc(mk[:, 3], [P, NT, NE], 2), ALU.is_equal))
                v.tensor_tensor(th[:].bitcast(BF16)[:, 0:NT * NE].rearrange("p (t e) -> p t e", t=NT), OH1, OH2,
                                ALU.add).then_inc(oh_ready, 1)
                dve.wait_ge(rank_fill, 1)
                v.tensor_copy(TOT_E, M[:].rearrange("p (t e) -> p e t", t=NT)).then_inc(rank_out, 1)

            flat = [P, NE, NT]
            by_expert = "p (e t) -> p e t"
            TOT_F, INC_F = bufs[4], bufs[5]
            TOT_E, INC_E, KEY_E = (w.rearrange(by_expert, e=NE) for w in (bufs[4], bufs[5], bufs[1]))

            def expert_starts():
                dve.wait_ge(rank_out, 1)
                link(v.tensor_tensor_scan(INC_F, bufs[6], TOT_F, 0.0, ALU.mult, ALU.add))
                link(v.tensor_copy(small[:, 0], INC_E[:, :, NT - 1]))
                link(v.tensor_tensor(KEY_E, bc(small[:, 0], flat, 2), bc(j128, flat, 1), ALU.is_gt))
                link(v.tensor_reduce(small[:, 1], KEY_E, AX.X, ALU.add))
                link(v.memset(small[:, 2], 1.0))
                link(v.tensor_tensor_scan(ends[:], small[:, 2], small[:, 1], 0.0, ALU.mult, ALU.add))
                link(v.tensor_tensor(small[:, 4], ends[:], small[:, 1], ALU.subtract))
                link(v.tensor_scalar(small[:, 5], small[:, 4], float(P), None, ALU.mult))
                dve.wait_ge(rank_fill, 2)
                v.tensor_copy(LOGIT, M[:].rearrange("p (t e) -> p t e", t=NT)).then_inc(rank_out, 1)

            def slots():
                dve.wait_ge(rank_out, 2)
                link(v.tensor_tensor(INC_E, INC_E, TOT_E, ALU.subtract))
                link(v.tensor_tensor(INC_E, INC_E, bc(small[:, 5], flat, 2), ALU.add))
                link(v.tensor_tensor(LOGIT, LOGIT, INC_E.rearrange("p e t -> p t e"), ALU.add))
                for c, oh in enumerate((OH1, OH2)):
                    link(v.tensor_tensor(KEY, oh, LOGIT, ALU.mult))
                    link(v.tensor_reduce(mk[:, 6], KEY, AX.X, ALU.add))
                    if c == 0:
                        link(v.tensor_copy(posu[:, c], mk[:, 6]))
                v.tensor_copy(posu[:, 1], mk[:, 6]).then_inc(routed, 1)

            def list_experts():
                size = [1, NSLOT_TILES, NE - 1]
                at_or_after = xy[0:1].rearrange("p a b d -> p (a b d)")[:, 0:NSLOT_TILES * (NE - 1)].rearrange(
                    "p (t e) -> p t e", e=NE - 1)
                link(v.tensor_tensor(at_or_after, bc(iot[0:1, :], size, 2), bc(ends[0:1, 0:NE - 1], size, 1), ALU.is_ge))
                link(v.tensor_reduce(count_of[:], at_or_after, AX.X, ALU.add))
                v.tensor_scalar(eid[:], count_of[:], float(WC), None, ALU.mult).then_inc(eid_ready, 1)

            def shares():
                dve.wait_ge(exp_dlt, 1)
                link(v.tensor_scalar(mk[:, 7], mk[:, 5], 1.0, None, ALU.add))
                link(v.reciprocal(w12[:, 0], mk[:, 7]))
                link(v.tensor_tensor(w12[:, 1], w12[:, 0], mk[:, 5], ALU.mult))
                list_experts()

            def bank_max(q, half, j):
                dve.wait_ge(score_done, 4 * q + j + 1)
                return v.tensor_reduce(mx4[:, half, j:j + 1], S[:, j], AX.X, ALU.max)

            def tile_max(q, half):
                dve.wait_ge(max4, q + 1)
                v.tensor_reduce(nmax[:, half:half + 1], mx4[:, half], AX.X, ALU.max, negate=True).then_inc(max_ready, 1)

            def prob_lo(n, half, j):
                cols = slice(half * P, (half + 1) * P)
                lo(n + j, j % 2, pTl[:, 4 * j:4 * j + 4, cols], pTh[:, 4 * j:4 * j + 4, cols])

            def stage(q, half, n):
                for j in range(2):
                    prob_lo(n, half, j)
                    bank_max(q + 1, 1 - half, j)
                bank_max(q + 1, 1 - half, 2)
                bank_max(q + 1, 1 - half, 3).then_inc(max4, 1)
                tile_max(q + 1, 1 - half)
                prob_lo(n, half, 2)

            def out_T(g):
                dve.wait_ge(pv_done, g + 1)
                v.tensor_copy(oT[:], O[:, 0:2 * P]).then_inc(oT_ready, 1)

            def combine(g, q):
                dve.wait_ge(exp_done, 4 * q + 8)
                v.tensor_reduce(den[:], dn[:, bass.ds(q, 2)], AX.X, ALU.add).then_inc(den_ready, 1)
                dve.wait_ge(den_ready, 2 * g + 1)
                v.reciprocal(rden[:], den[:]).then_inc(den_ready, 1)
                dve.wait_ge(den_ready, 2 * g + 2)
                dve.wait_ge(back_done, g + 1)
                dve.wait_ge(sg_ready, g + 1)
                for a in range(2):
                    ins = v.scalar_tensor_tensor(out=sg[:, a], in0=O[:, (2 + a) * P:(3 + a) * P], scalar=rden[:, a:a + 1],
                                                 in1=sg[:, a], op0=ALU.mult, op1=ALU.add)
                ins.then_inc(pre_ready, 1)

            def add_experts(dst, side, t, k, half_base, done):
                for c in range(2):
                    for a in range(2):
                        ins = v.scalar_tensor_tensor(out=dst[:, a], in0=xy[:, side, 2 * a + c],
                                                     scalar=w12[:, c, bass.ds(t + a, 1)], in1=dst[:, a],
                                                     op0=ALU.mult, op1=ALU.add)
                    if c == 0:
                        ins.then_inc(ffn_half, 1)
                        dve.wait_ge(ffn_half, 2 * k + half_base + 1)
                ins.then_inc(done, 1)

            def base(b, i):
                if b == 0:
                    return
                last = isinstance(i, int) and i == NP - 1
                if last:
                    dve.wait_ge(last_in, 32)
                else:
                    dve.wait_ge(rb_in, 16 * (i + 1))
                if last:
                    dve.wait_ge(gat_last, 128)
                else:
                    dve.wait_ge(gat_a, 64 * (i + 1))
                add_experts(rb_last if last else rb, 2 if last else 0, 2 * i, i, 0, rb_ready)
                if not last:
                    dve.wait_ge(xb_in, 16 * (i + 1) + 16 * NP)
                    dve.wait_ge(gat_b, 64 * (i + 1))
                add_experts(xb_last if last else xb, 3 if last else 1, 2 * i + TB, i, 1, base_ready)

            def attention(b):
                q0, g0, n0 = b * TB, b * NP, T_ATT[b]
                if b == 0:
                    for j in range(4):
                        ins = bank_max(q0, 0, j)
                    ins.then_inc(max4, 1)
                    tile_max(q0, 0)
                if b == 0:
                    first_choice(1)
                stage(q0, 0, n0)
                energy_lo(g0 + 1)
                prob_lo(n0, 0, 3)

                def pair(i, first=False, last=False, route=None):
                    stage(q0 + 2 * i + 1, 1, n0 + 8 * i + 4)
                    prob_lo(n0 + 8 * i + 4, 1, 3)
                    if not first:
                        base(b, i - 1)
                    if route:
                        route()
                    stage(q0 + 2 * i + 2, 0, n0 + 8 * i + 8)
                    if not last:
                        energy_lo(g0 + i + 2)
                    out_T(g0 + i)
                    prob_lo(n0 + 8 * i + 8, 0, 3)
                    combine(g0 + i, q0 + 2 * i)

                routes = (second_choice, choices, expert_starts, slots, shares) if b == 0 else (None,)
                for i, route in enumerate(routes):
                    pair(i, first=i == 0, route=route)
                if len(routes) < NP - 2:
                    with dve.Fori(len(routes), NP - 2) as i:
                        pair(i)
                pair(NP - 2, last=True)
                i = NP - 1
                for j in range(4):
                    prob_lo(n0 + 8 * i + 4, 1, j)
                base(b, i - 1)
                base(b, i)
                out_T(g0 + i)
                combine(g0 + i, q0 + 2 * i)

            copy_logits(1)
            attention(0)

            tokens_lo(0, T_PRO[1])
            tokens_lo(1, T_PRO[1] + 1)
            for c in range(CB):
                spin_lo(1, c)
                if c + 2 < CB:
                    tokens_lo(c + 2, T_PRO[1] + c + 2)
            energy_lo(NP)
            dve.wait_ge(back_done, NP)
            mean_step(1)
            for c in range(CB):
                row_lo(1, c)

            def gate_up(g, u):
                dve.wait_ge(gu_done, g + 1)
                t3 = S[:, 2 * u:2 * u + 2].rearrange("p b (a f s) -> p (b a) f s", a=2, s=2)
                gate, up = (gu_sb[:, u, s].rearrange("p (a f) -> p a f", a=4) for s in range(2))
                v.tensor_scalar(gate, t3[:, :, :, 0], LIMIT, 0.5, ALU.min, ALU.mult).then_inc(gate_ready, 1)
                v.tensor_scalar(up, t3[:, :, :, 1], 1.0 - LIMIT, 1.0 + LIMIT, ALU.max, ALU.min).then_inc(up_ready, 1)

            def gated(g, u):
                dve.wait_ge(th_ready, g + 1)
                dve.wait_ge(au_ready, g + 1)
                v.scalar_tensor_tensor(out=gu_sb[:, u, 1], in0=th[:], scalar=1.0, in1=gu_sb[:, u, 1],
                                       op0=ALU.add, op1=ALU.mult).then_inc(ga_ready, 1)

            def rows_lo(n, bank, u):
                lo(n, bank, xT[u][1], xT[u][0])

            def gated_lo(n, bank, u):
                lo(n, bank, gT[u][1], gT[u][0])

            def expert_step(g, u, rows=True):
                if rows:
                    rows_lo(T_MOE + 2 * g, 0, 1 - u)
                gated(g - 1, 1 - u)
                gate_up(g, u)
                gated_lo(T_MOE + 2 * g + (1 if rows else 0), 1 if rows else 0, 1 - u)

            rows_lo(T_MOE, 0, 0)
            rows_lo(T_MOE + 1, 1, 1)
            gate_up(0, 0)
            expert_step(1, 1)
            with dve.Fori(1, NG // 2 - 1) as j:
                expert_step(2 * j, 0)
                expert_step(2 * j + 1, 1)
            expert_step(NG - 2, 0)
            expert_step(NG - 1, 1, rows=False)
            gated(NG - 1, 1)
            bank_max(TB, 0, 0)
            bank_max(TB, 0, 1)
            gated_lo(T_MOE + 2 * NG - 1, 1, 1)
            bank_max(TB, 0, 2)
            bank_max(TB, 0, 3).then_inc(max4, 1)
            tile_max(TB, 0)

            attention(1)


_INS = ["L0_attn_x", "L0_attn_W_spin", "L0_attn_b_spin", "L0_attn_W_global", "L0_attn_W_J", "L0_attn_beta",
        "L0_ffn_Wg", "L0_ffn_bg", "L0_ffn_Wgu", "L0_ffn_bgu", "L0_ffn_Wd", "L0_ffn_bd"]


def kernel(**inputs):
    import numpy as _np
    import concourse.bacc as _bacc
    from concourse import mybir as _mybir
    from concourse.bass_utils import run_bass_kernel_spmd as _run

    nc = _bacc.Bacc("TRN2", target_bir_lowering=False, num_devices=1)
    arrays, args = {}, []
    for name in _INS:
        a = _np.ascontiguousarray(inputs[name])
        arrays[f"in_{name}"] = a
        args.append(nc.dram_tensor(f"in_{name}", a.shape, _mybir.dt.from_np(a.dtype), kind="ExternalInput").ap())
    shape = inputs["L0_attn_x"].shape
    args.append(nc.dram_tensor("out_y", shape, _mybir.dt.float32, kind="ExternalOutput").ap())
    build(nc, *args)
    r = _run(nc, [arrays], core_ids=[0])
    return r.results[0]["out_y"]
```

```python
from contextlib import ExitStack

import concourse.bass as bass
from concourse import mybir

F32 = mybir.dt.float32
F32R = mybir.dt.float32r
BF16 = mybir.dt.bfloat16
U32 = mybir.dt.uint32
I32 = mybir.dt.int32
ALU = mybir.AluOpType
ACT = mybir.ActivationFunctionType
AX = mybir.AxisListType

P = 128
EPS = 1e-5
LIMIT = 7.0
ALPHA = 1.702


def build(nc, x, W_spin, b_spin, W_global, W_J, beta, Wg, bg, Wgu, bgu, Wd, bd, out):
    NB, N, D = x.shape
    NE, _, F2 = Wgu.shape
    F = F2 // 2
    assert D == P and F == P and N % 512 == 0
    TB = N // P
    NT = NB * TB
    CB = TB // 4
    NCH = NT // 4
    NP = TB // 2
    NSLOT_TILES = 2 * NT + NE
    NG = NSLOT_TILES // 4
    WC = F2 + D
    SCALE = 1.0 / float(D) ** 0.5
    BIG = 3.0e38
    ROUTED_BY = 3
    SCATTER_AT = (0, 7, 13, 19, 25, 32)
    assert SCATTER_AT[-1] == NT and len(SCATTER_AT) == NP - ROUTED_BY + 1
    assert NSLOT_TILES % 8 == 0 and NB == 2 and NE * NT == 512

    x_v = x.rearrange("b (p t) d -> b p t d", p=P)
    out_v = out.rearrange("b (p t) d -> b p t d", p=P)
    slots_x = nc.dram_tensor("slots_x", [NSLOT_TILES * P, D], F32, kind="Internal").ap()
    slots_y = nc.dram_tensor("slots_y", [NSLOT_TILES * P, D], F32, kind="Internal").ap()
    part = nc.dram_tensor("part", [P, TB, D], F32, kind="Internal").ap()
    bias_parts = nc.dram_tensor("bias_parts", [2, NE, WC], F32, kind="Internal").ap()
    slots_x_v = slots_x.rearrange("(s p) d -> p s d", p=P)
    slots_y_v = slots_y.rearrange("(s p) d -> p s d", p=P)

    with ExitStack() as ctx:
        def sb(name, shape, dt=F32):
            return ctx.enter_context(nc.sbuf_tensor(name, shape, dt))

        def ps(name, shape):
            return ctx.enter_context(nc.psum_tensor(name, shape, F32))

        def sem(name):
            return ctx.enter_context(nc.semaphore(name))

        xn = sb("xn", [P, NT, D])
        sTh, sTl = sb("sTh", [P, N], F32R), sb("sTl", [P, N], F32R)
        sh, sl = sb("sh", [P, TB, D], F32R), sb("sl", [P, TB, D], F32R)
        prob = sb("prob", [P, 2, N])
        pTh, pTl = sb("pTh", [P, TB, 2 * P], F32R), sb("pTl", [P, TB, 2 * P], F32R)
        wh, wl = sb("wh", [P, NE, WC], F32R), sb("wl", [P, NE, WC], F32R)
        wb = sb("wb", [P, NE, WC], F32R)
        eTh, eTl = sb("eTh", [P, 2 * P], F32R), sb("eTl", [P, 2 * P], F32R)
        oT = sb("oT", [P, 2 * P])
        gu_sb = sb("gu_sb", [P, 2, 2, 512])
        th = sb("th", [P, 512])
        xy = sb("xy", [P, 4, 4, D])
        sg = sb("sg", [P, 2, D])
        xb = sb("xb", [P, 2, D])
        rb = sb("rb", [P, 2, D])
        ident = sb("ident", [P, P])
        identr = sb("identr", [P, P], F32R)
        onesr = sb("onesr", [P, P], F32R)
        tri = sb("tri", [P, P], BF16)
        onesb = sb("onesb", [P, P], BF16)
        wspTh, wspTl = sb("wspTh", [P, P], F32R), sb("wspTl", [P, P], F32R)
        wjTh, wjTl = sb("wjTh", [P, P], F32R), sb("wjTl", [P, P], F32R)
        wglT = sb("wglT", [P, P])
        wgT2 = sb("wgT2", [P, 2 * NE], F32R)
        wgTh, wgTl = wgT2[:, 0:NE], wgT2[:, NE:2 * NE]
        gb = sb("gb", [P, D])
        bspin = sb("bspin", [P, 1])
        betac = sb("betac", [P, 1])
        bgr = sb("bgr", [P, NE])
        stats = sb("stats", [P, NT, 6])
        mv = sb("mv", [P, NT, 2])
        rstd = sb("rstd", [P, NT])
        shift = sb("shift", [P, NT])
        epsc = sb("epsc", [P, 1])
        msum = sb("msum", [P, CB + 1])
        mx4 = sb("mx4", [P, 2, 4])
        nmax = sb("nmax", [P, 2])
        dn = sb("dn", [P, NT, 4])
        den = sb("den", [P, 2])
        rden = sb("rden", [P, 2])
        iot = sb("iot", [P, NSLOT_TILES], I32)
        w12 = sb("w12", [P, 2, NT])
        posu = sb("posu", [P, 2, NT], U32)
        ends = sb("ends", [P, NE])
        count_of = sb("count_of", [1, NSLOT_TILES])
        eid = sb("eid", [1, NSLOT_TILES], I32)
        pTh_flat, pTl_flat = (w[:].rearrange("p a b -> p (a b)") for w in (pTh, pTl))

        def part_slot(k):
            return tuple(w[:, 512 * k:512 * k + 512].rearrange("p (a b) -> p a b", a=4) for w in (pTh_flat, pTl_flat))

        xT = [part_slot(k) for k in range(4)]
        gT = [part_slot(2), part_slot(3)]
        b_hl = tuple(w[0:NE, 2048:2048 + WC] for w in (pTh_flat, pTl_flat))
        xb_last = gu_sb[:, 0, 0].rearrange("p (a d) -> p a d", a=4)[:, 0:2]
        rb_last = gu_sb[:, 0, 0].rearrange("p (a d) -> p a d", a=4)[:, 2:4]
        mk = rb[:].rearrange("p a b -> p (a b)").rearrange("p (k t) -> p k t", t=NT)
        bufs = [gu_sb[:, a, c] for a in range(2) for c in range(2)]
        bufs += [xy[:, a].rearrange("p b d -> p (b d)") for a in range(4)]
        LOGIT, KEY, OH1, OH2, TOT, INC = (w.rearrange("p (t e) -> p t e", t=NT) for w in bufs[0:6])
        MASK = bufs[6].rearrange("p (e t) -> p e t", e=NE)
        small = bufs[7][:, 0:5 * NE].rearrange("p (k e) -> p k e", e=NE)
        rev, j128 = bufs[7][:, 5 * NE:6 * NE], bufs[7][:, 6 * NE:6 * NE + NT]
        w4_st = gu_sb[:, 0].rearrange("p a n -> p (a n)")[:, 0:4 * P].rearrange("p (a n) -> p a n", a=4)
        b_st = gu_sb[0:NE, 1].rearrange("p a n -> p (a n)")[:, 0:WC]
        b_ad = th[0:NE, 0:WC]

        S = ps("S", [P, 4, 512])
        T = ps("T", [P, 2, 512])
        O = ps("O", [P, 512])
        M = ps("M", [P, 512])

        def spin_bank(c):
            return (M[:], S[:, 0], S[:, 1], O[:])[c]

        def row_bank(b, c):
            return ((O[:], M[:], O[:], O[:]), (S[:, 0], S[:, 1], O[:], M[:]))[b][c]

        ld_x = [sem(f"ld_x{c}") for c in range(NCH)]
        ld_w, ld_b = sem("ld_w"), sem("ld_b")
        ld_gu, ld_d = sem("ld_gu"), sem("ld_d")
        consts = sem("consts")
        route_consts = sem("route_consts")
        zeroed = sem("zeroed")
        dchain = sem("dchain")
        rstd_in, rstd_mid = sem("rstd_in"), sem("rstd_mid")
        rstd_ready = sem("rstd_ready")
        xn_ready = [sem("xn_ready0"), sem("xn_ready1")]
        wt_turned, wt_hi, wt_done = sem("wt_turned"), sem("wt_hi"), sem("wt_done")
        t_fill, t_hi, t_lo = sem("t_fill"), sem("t_hi"), sem("t_lo")
        m_fill, m_hi, m_lo = sem("m_fill"), sem("m_hi"), sem("m_lo")
        r_fill, r_hi, r_lo = sem("r_fill"), sem("r_hi"), sem("r_lo")
        e_fill, e_hi, e_lo = sem("e_fill"), sem("e_hi"), sem("e_lo")
        mean_ready, g_done, g_ready = sem("mean_ready"), sem("g_done"), sem("g_ready")
        log_done, log_out = sem("log_done"), sem("log_out")
        dlt, exp_dlt = sem("dlt"), sem("exp_dlt")
        oh_ready, rank_fill, rank_out = sem("oh_ready"), sem("rank_fill"), sem("rank_out")
        routed, eid_ready = sem("routed"), sem("eid_ready")
        w_hi, w_lo = sem("w_hi"), sem("w_lo")
        b_adj, b_hi, b_lo = sem("b_adj"), sem("b_hi"), sem("b_lo")
        wb_clear, b_out, b_in = sem("wb_clear"), sem("b_out"), sem("b_in")
        score_done = sem("score_done")
        max4 = sem("max4")
        max_ready = sem("max_ready")
        exp_done = sem("exp_done")
        pv_done, oT_ready, back_done = sem("pv_done"), sem("oT_ready"), sem("back_done")
        den_ready, pre_ready = sem("den_ready"), sem("pre_ready")
        tanh_ready = sem("tanh_ready")
        sg_half, sg_ready, fin_ready = sem("sg_half"), sem("sg_ready"), sem("fin_ready")
        xb_in, xb_out = sem("xb_in"), sem("xb_out")
        rb_in, rb_out = sem("rb_in"), sem("rb_out")
        rb_ready, base_ready = sem("rb_ready"), sem("base_ready")
        ffn_half = sem("ffn_half")
        scat = sem("scat")
        gat_a, gat_b = sem("gat_a"), sem("gat_b")
        gat_last = sem("gat_last")
        last_in = sem("last_in")
        xg_in = [sem("xg_in0"), sem("xg_in1")]
        y_out = [sem("y_out0"), sem("y_out1")]
        gu_done, y_done = sem("gu_done"), sem("y_done")
        gate_ready, up_ready, ga_ready = sem("gate_ready"), sem("up_ready"), sem("ga_ready")
        th_ready, au_ready, y_ready = sem("th_ready"), sem("au_ready"), sem("y_ready")

        T_ATT_0 = NCH
        T_PRO_1 = T_ATT_0 + 4 * TB
        T_MOE = T_PRO_1 + CB
        T_ATT = [T_ATT_0, T_MOE + 2 * NG]

        def rows_fill(g):
            return T_MOE + (g if isinstance(g, int) and g < 2 else 2 * g - 2)

        def gated_fill(g):
            if isinstance(g, int) and g >= NG - 2:
                return T_MOE + g + NG
            return T_MOE + 2 * g + 3

        def bc(ap, shape, at):
            return ap.unsqueeze(at).broadcast_to(shape)

        block = ctx.enter_context(nc.Block())

        @block.sync
        def _(sp):
            with nc.allow_non_contiguous_dma(reason="small vectors"):
                def load_x(c):
                    b, t = c // CB, 4 * (c % CB)
                    sp.dma_start(xn[:, 4 * c:4 * c + 4], x_v[b][:, t:t + 4]).then_inc(ld_x[c], 16)

                load_x(0)
                load_x(1)
                sp.dma_start(w4_st[:, 0], W_spin).then_inc(ld_w, 16)
                sp.dma_start(w4_st[:, 1], W_J).then_inc(ld_w, 16)
                sp.dma_start(w4_st[:, 2], W_global).then_inc(ld_w, 16)
                sp.dma_start(w4_st[0:NE, 3], Wg).then_inc(ld_w, 16)
                sp.dma_start(bspin[:], b_spin.unsqueeze(1)).then_inc(ld_w, 16)
                sp.dma_start(betac[:], beta.partition_broadcast(P)).then_inc(ld_w, 16)
                sp.dma_start(bgr[:], bg.partition_broadcast(P)).then_inc(ld_w, 16)
                load_x(2)
                load_x(3)
                sp.dma_start(b_st[:, 0:F2], bgu).then_inc(ld_b, 16)
                sp.dma_start(b_st[:, F2:WC], bd).then_inc(ld_b, 16)
                for c in range(CB, NCH):
                    load_x(c)
                sp.dma_start(wl[:, :, F2:WC].bitcast(F32), Wd.rearrange("e k n -> k e n")).then_inc(ld_d, 16)
                sp.dma_start(wl[:, :, 0:F2].bitcast(F32), Wgu.rearrange("e k n -> k e n")).then_inc(ld_gu, 16)
                sp.wait_ge(consts, 2)
                sp.dma_start(
                    slots_x.rearrange("(p r) d -> p (r d)", p=P).rearrange("p (a n) -> p a n", n=2 * D),
                    bc(xb[:].rearrange("p a d -> p (a d)"), [P, NSLOT_TILES // 2, 2 * D], 1)).then_inc(zeroed, 16)
                sp.wait_ge(b_hi, 1)
                sp.dma_start(bias_parts[0], b_hl[0].bitcast(F32)).then_inc(b_out, 16)
                sp.wait_ge(b_lo, 1)
                sp.dma_start(bias_parts[1], b_hl[1].bitcast(F32)).then_inc(b_out, 16)
                sp.wait_ge(b_out, 32)
                sp.wait_ge(wb_clear, 1)
                sp.dma_start(wb[0:2].bitcast(F32), bias_parts).then_inc(b_in, 16)
                sp.wait_ge(zeroed, 16)
                def base_pair(k):
                    if not (isinstance(k, int) and k == 0):
                        sp.wait_ge(xb_out, k * 16)
                    sp.dma_start(xb[:], x_v[0][:, bass.ds(2 * k, 2)]).then_inc(xb_in, 16)
                    sp.wait_ge(fin_ready, k + 1)
                    sp.dma_start(part[:, bass.ds(2 * k, 2)], xb[:]).then_inc(xb_out, 16)

                base_pair(0)
                with sp.Fori(1, NP) as k:
                    base_pair(k)
                sp.wait_ge(scat, 16 * 2 * NT)
                for u in range(2):
                    sp.dma_start(xy[:, u], slots_x_v[:, 4 * u:4 * u + 4]).then_inc(xg_in[u], 16)

                def rows_in(g, u):
                    sp.wait_ge(t_fill, rows_fill(g) + 1)
                    sp.dma_start(xy[:, u], slots_x_v[:, bass.ds(4 * g + 8, 4)]).then_inc(xg_in[u], 16)

                def results_out(g, u):
                    sp.wait_ge(y_ready, g - 1)
                    sp.dma_start(slots_y_v[:, bass.ds(4 * g - 8, 4)], xy[:, 2 + u]).then_inc(y_out[u], 16)

                rows_in(0, 0)
                rows_in(1, 1)
                with sp.Fori(1, NG // 2 - 1) as j:
                    for u in range(2):
                        rows_in(2 * j + u, u)
                        results_out(2 * j + u, u)
                for g in range(NG - 2, NG + 2):
                    results_out(g, g % 2)
                sp.wait_ge(y_ready, NG)
                sp.dma_start(xb_last, x_v[1][:, TB - 2:TB]).then_inc(last_in, 16)
                sp.wait_ge(xb_out, NP * 16)
                sp.dma_start(rb_last, part[:, TB - 2:TB]).then_inc(last_in, 16)
                for k in range(NP):
                    last = k == NP - 1
                    if not last:
                        sp.wait_ge(xb_out, k * 16 + NP * 16)
                        sp.dma_start(xb[:], x_v[1][:, 2 * k:2 * k + 2]).then_inc(xb_in, 16)
                        if k:
                            sp.wait_ge(rb_out, k * 16)
                        sp.dma_start(rb[:], part[:, 2 * k:2 * k + 2]).then_inc(rb_in, 16)
                    sp.wait_ge(rb_ready, k + 1)
                    sp.dma_start(out_v[0][:, 2 * k:2 * k + 2], rb_last if last else rb[:]).then_inc(rb_out, 16)
                    sp.wait_ge(fin_ready, k + 1 + NP)
                    sp.dma_start(out_v[1][:, 2 * k:2 * k + 2], xb_last if last else xb[:]).then_inc(xb_out, 16)
                sp.wait_ge(xb_out, 2 * NP * 16)
                sp.wait_ge(rb_out, NP * 16)

        @block.gpsimd
        def _(pool):
            nc.gpsimd.memset(xb[:], 0.0).then_inc(consts, 1)
            nc.gpsimd.memset(ident[:], 0.0).then_inc(consts, 1)
            nc.gpsimd.memset(tri[:], 1.0).then_inc(consts, 1)
            nc.gpsimd.memset(onesb[:], 1.0).then_inc(consts, 1)
            nc.gpsimd.iota(iot[:], [[1, NSLOT_TILES]], base=0, channel_multiplier=0).then_inc(consts, 1)
            nc.gpsimd.memset(epsc[:], EPS).then_inc(consts, 1)
            nc.gpsimd.memset(onesr[:].bitcast(F32), 1.0).then_inc(consts, 1)
            pool.wait_ge(consts, 7)
            nc.gpsimd.affine_select(out=ident[:], in_=ident[:], compare_op=ALU.not_equal, fill=1.0, base=0,
                                    pattern=[[-1, P]], channel_multiplier=1).then_inc(consts, 1)
            nc.gpsimd.affine_select(out=tri[:], in_=tri[:], compare_op=ALU.is_gt, fill=0.0, base=0,
                                    pattern=[[1, P]], channel_multiplier=-1).then_inc(consts, 1)
            nc.gpsimd.memset(MASK, 1.0).then_inc(route_consts, 1)
            nc.gpsimd.tensor_scalar(rev, iot[:, 0:NE], -1.0, float(NE), ALU.mult, ALU.add).then_inc(route_consts, 1)
            nc.gpsimd.tensor_scalar(j128, iot[:, 0:NT], float(P), None, ALU.mult).then_inc(route_consts, 1)
            pool.wait_ge(route_consts, 1)
            nc.gpsimd.memset(MASK[:, :, 0:1], 0.0).then_inc(route_consts, 1)
            nc.gpsimd.memset(wb[:].bitcast(F32), 0.0).then_inc(wb_clear, 1)

            pool.wait_ge(ld_d, 16)
            pool.wait_ge(ld_gu, 16)

            def cut_weights(k):
                part = slice(k * NE // 4, (k + 1) * NE // 4)
                nc.gpsimd.tensor_copy(wh[:, part], wl[:, part].bitcast(F32)).then_inc(w_hi, 1)
                pool.wait_ge(w_hi, k + 1)
                nc.gpsimd.tensor_tensor(wl[:, part], wl[:, part].bitcast(F32), wh[:, part].bitcast(F32),
                                        ALU.subtract).then_inc(w_lo, 1)

            def fin(g):
                pool.wait_ge(tanh_ready, g + 1)
                if g < NP:
                    pool.wait_ge(xb_in, 16 * (g + 1))
                else:
                    pool.wait_ge(base_ready, g + 1 - NP)
                total = xb_last if g == 2 * NP - 1 else xb[:]
                nc.gpsimd.tensor_tensor(total, total, sg[:], ALU.add).then_inc(fin_ready, 1)

            def sg_step(g):
                k = g % NP
                if g:
                    pool.wait_ge(fin_ready, g)
                if k == 0:
                    pool.wait_ge(r_lo, (g // NP + 1) * CB)
                    pool.wait_ge(g_ready, g // NP + 1)
                nc.gpsimd.tensor_tensor(sg[:], sh[:, 2 * k:2 * k + 2].bitcast(F32), sl[:, 2 * k:2 * k + 2].bitcast(F32),
                                        ALU.add).then_inc(sg_half, 1)
                pool.wait_ge(sg_half, g + 1)
                nc.gpsimd.tensor_tensor(sg[:], sg[:], bc(gb[:], [P, 2, D], 1), ALU.add).then_inc(sg_ready, 1)

            def scatter(first, last):
                for c in range(2):
                    if first == 0:
                        pool.wait_ge(routed, c + 1)
                    for t in range(first, last):
                        pool.indirect_dma_start(slots_x, bass.IndirectOffsetOnAxis(ap=posu[:, c, t:t + 1], axis=0),
                                                xn[:, t], None).then_inc(scat, 16)

            for k in range(NP):
                if k:
                    fin(k - 1)
                sg_step(k)
                for quarter in ((0,), (1, 2), (3,), ())[min(k, 3)]:
                    cut_weights(quarter)
                if k == ROUTED_BY:
                    pool.wait_ge(zeroed, 16)
                if k >= ROUTED_BY:
                    scatter(SCATTER_AT[k - ROUTED_BY], SCATTER_AT[k - ROUTED_BY + 1])
            fin(NP - 1)
            with pool.Fori(0, NG // 2) as j:
                for u in range(2):
                    pool.wait_ge(up_ready, 2 * j + u + 1)
                    pool.wait_ge(gate_ready, 2 * j + u + 1)
                    nc.gpsimd.tensor_tensor(gu_sb[:, u, 1], gu_sb[:, u, 1], gu_sb[:, u, 0], ALU.mult).then_inc(au_ready, 1)
            pool.wait_ge(y_out[0], 16 * (NG // 2))
            pool.wait_ge(y_out[1], 16 * (NG // 2))

            def gather(side, t, c, done):
                pool.indirect_dma_start(xy[:, side, 2 * (t % 2) + c], None, slots_y,
                                        bass.IndirectOffsetOnAxis(ap=posu[:, c, t:t + 1], axis=0)).then_inc(done, 16)

            for k in range(NP):
                if k:
                    fin(NP + k - 1)
                sg_step(NP + k)
                if k < NP - 1:
                    for side, (done, t0) in enumerate(((gat_a, 2 * k), (gat_b, TB + 2 * k))):
                        if k:
                            pool.wait_ge(rb_ready if side == 0 else base_ready, k)
                        for t in range(2):
                            for c in range(2):
                                gather(side, t0 + t, c, done)
                if NP - 5 <= k < NP - 1:
                    t = k - (NP - 5)
                    for c in range(2):
                        gather(2 + t // 2, (t // 2) * TB + TB - 2 + t % 2, c, gat_last)
            fin(2 * NP - 1)

        @block.tensor
        def _(pe):
            def three(o, ah, al, bh, bl, start=True, stop=True):
                nc.tensor.matmul(o, ah, bh, start=start, stop=False)
                nc.tensor.matmul(o, ah, bl, start=False, stop=False)
                return nc.tensor.matmul(o, al, bh, start=False, stop=stop)

            def t_free(n):
                if not isinstance(n, int) or n >= 2:
                    pe.wait_ge(t_lo, n - 1)

            def turn(n, tile, parity, ready=None):
                t_free(n)
                for a in range(4):
                    m = nc.tensor.transpose(T[:, parity, a * P:(a + 1) * P], tile(a), ident[:])
                m.then_inc(t_fill, 1)

            pe.wait_ge(consts, 9)
            pe.wait_ge(ld_w, 112)
            for a in range(3):
                nc.tensor.transpose(S[:, 0, a * P:(a + 1) * P], w4_st[:, a], ident[:])
            nc.tensor.transpose(S[:, 0, 3 * P:3 * P + NE], w4_st[0:NE, 3], ident[0:NE, 0:NE]).then_inc(wt_turned, 1)

            def spin(c):
                xh, xl = xT[c % 4]
                three(spin_bank(c), wspTh[:], wspTl[:], flat(xh), flat(xl)).then_inc(m_fill, 1)

            def flat(ap):
                return ap.rearrange("p a b -> p (a b)")

            def turn_tokens(b, c, n):
                pe.wait_ge(xn_ready[b], c + 1)
                turn(n, lambda a: xn[:, b * TB + 4 * c + a], n % 2)

            def energy(i):
                lo, hi = sTl[:, bass.ds(i * 2 * P, 2 * P)], sTh[:, bass.ds(i * 2 * P, 2 * P)]
                three(M[:, 0:2 * P], wjTh[:], wjTl[:], hi, lo).then_inc(e_fill, 1)

            def row_of_s(b, c):
                for a in range(4):
                    o = row_bank(b, c)[:, a * P:(a + 1) * P]
                    nc.tensor.matmul(o, sTh[:, (4 * c + a) * P:(4 * c + a + 1) * P], identr[:], start=True, stop=False)
                    m = nc.tensor.matmul(o, sTl[:, (4 * c + a) * P:(4 * c + a + 1) * P], identr[:], start=False, stop=True)
                m.then_inc(r_fill, 1)

            turn_tokens(0, 0, 0)
            turn_tokens(0, 1, 1)
            pe.wait_ge(wt_done, 1)
            for c in range(NCH):
                pe.wait_ge(t_lo, c + 1)
                if c < CB:
                    spin(c)
                if c + 2 < NCH:
                    turn_tokens((c + 2) // CB, (c + 2) % CB, c + 2)
                if c == CB:
                    pe.wait_ge(m_lo, CB)
                    energy(0)
                xh, xl = xT[c % 4]
                for a in range(4):
                    o = S[:, 2:4].rearrange("p b n -> p (b n)")[:, (4 * c + a) * 2 * NE:(4 * c + a + 1) * 2 * NE]
                    nc.tensor.matmul(o, xh[:, a], wgT2[:], start=True, stop=False)
                    m = nc.tensor.matmul(o[:, 0:NE], xl[:, a], wgT2[:, 0:NE], start=False, stop=True)
                m.then_inc(log_done, 1)

            def global_row(b):
                pe.wait_ge(mean_ready, b + 1)
                nc.tensor.matmul(O[:, 0:D], mean_bc, wglT[:], start=True, stop=True).then_inc(g_done, 1)

            mean_bc = oT[:, 0:P]
            ohb = th[:].bitcast(BF16)[:, 0:NT * NE]

            def count_pairs(k):
                if k == 0:
                    pe.wait_ge(oh_ready, 1)
                nc.tensor.matmul(M[:], (onesb, tri)[k][:], ohb, start=True, stop=True).then_inc(rank_fill, 1)

            def score(q, half, j):
                if not (isinstance(q, int) and q == 0):
                    pe.wait_ge(exp_done, 4 * q - 4 + j + 1)
                e_h, e_l = eTh[:, half * P:(half + 1) * P], eTl[:, half * P:(half + 1) * P]
                three(S[:, j], e_h, e_l, sTh[:, 512 * j:512 * j + 512],
                      sTl[:, 512 * j:512 * j + 512]).then_inc(score_done, 1)

            def turn_prob(q, half, n, j):
                t_free(n + j)
                pe.wait_ge(exp_done, 4 * q + j + 1)
                for a in range(4):
                    m = nc.tensor.transpose(T[:, j % 2, a * P:(a + 1) * P],
                                            prob[:, half, (4 * j + a) * P:(4 * j + a + 1) * P], ident[:])
                m.then_inc(t_fill, 1)

            def stage(q, half, n, first=0):
                for j in range(first, 4):
                    turn_prob(q, half, n, j)
                    score(q + 1, 1 - half, j)

            def values(n, first, last):
                for t in range(first, last):
                    if t % 4 == 0:
                        pe.wait_ge(t_lo, n + 4 + t // 4 + 1)
                    m = three(O[:, 0:2 * P], sh[:, t], sl[:, t], pTh[:, t], pTl[:, t], start=t == 0, stop=t == TB - 1)
                if last == TB:
                    m.then_inc(pv_done, 1)

            def turn_back(g):
                pe.wait_ge(oT_ready, g + 1)
                nc.tensor.transpose(O[:, 2 * P:3 * P], oT[:, 0:P], ident[:])
                nc.tensor.transpose(O[:, 3 * P:4 * P], oT[:, P:2 * P], ident[:]).then_inc(back_done, 1)

            def attention(b):
                q0, g0, n0 = b * TB, b * NP, T_ATT[b]
                if b == 0:
                    pe.wait_ge(e_lo, 1)
                    score(q0, 0, 0)
                    score(q0, 0, 1)
                    pe.wait_ge(log_out, 2)
                    score(q0, 0, 2)
                    score(q0, 0, 3)
                    row_of_s(0, 0)
                    row_of_s(0, 1)
                stage(q0, 0, n0)
                if b == 0:
                    pe.wait_ge(r_lo, 2)
                energy(1)
                if b == 0:
                    row_of_s(0, 2)
                turn_prob(q0 + 1, 1, n0 + 4, 0)
                pe.wait_ge(e_lo, g0 + 2)
                score(q0 + 2, 0, 0)
                if b == 0:
                    pe.wait_ge(r_lo, 3)
                    row_of_s(0, 3)
                    pe.wait_ge(r_lo, 4)
                    global_row(0)

                def pair(i, last=False):
                    stage(q0 + 2 * i + 1, 1, n0 + 8 * i + 4, first=1)
                    if b == 0 and isinstance(i, int) and i == 2:
                        count_pairs(1)
                    if isinstance(i, int) and i == 0:
                        pe.wait_ge(g_ready, b + 1)
                    values(n0 + 8 * i, 0, 8)
                    if b == 0 and isinstance(i, int) and i == 1:
                        count_pairs(0)
                    values(n0 + 8 * i, 8, TB - 4)
                    stage(q0 + 2 * i + 2, 0, n0 + 8 * i + 8)
                    if b == 0 and isinstance(i, int) and i in (1, 2):
                        pe.wait_ge(rank_out, i)
                    if not last:
                        energy(i + 2)
                    values(n0 + 8 * i, TB - 4, TB)
                    turn_prob(q0 + 2 * i + 3, 1, n0 + 8 * i + 12, 0)
                    turn_back(g0 + i)
                    if not last:
                        pe.wait_ge(e_lo, g0 + i + 3)
                        score(q0 + 2 * i + 4, 0, 0)

                straight = 3 if b == 0 else 1
                for i in range(straight):
                    pair(i)
                with pe.Fori(straight, NP - 2) as i:
                    pair(i)
                pair(NP - 2, last=True)
                i = NP - 1
                for j in range(1, 4):
                    turn_prob(q0 + 2 * i + 1, 1, n0 + 8 * i + 4, j)
                values(n0 + 8 * i, 0, TB)
                turn_back(g0 + i)

            attention(0)

            pe.wait_ge(exp_done, 4 * TB)
            pe.wait_ge(pre_ready, NP)
            turn_tokens(1, 0, T_PRO_1)
            turn_tokens(1, 1, T_PRO_1 + 1)
            for c in range(CB):
                pe.wait_ge(t_lo, T_PRO_1 + c + 1)
                spin(c)
                if c + 2 < CB:
                    turn_tokens(1, c + 2, T_PRO_1 + c + 2)
            pe.wait_ge(m_lo, CB + 2)
            row_of_s(1, 0)
            pe.wait_ge(m_lo, CB + 3)
            row_of_s(1, 1)
            energy(0)
            pe.wait_ge(m_lo, 2 * CB)
            row_of_s(1, 2)
            pe.wait_ge(e_lo, NP + 1)
            row_of_s(1, 3)
            pe.wait_ge(r_lo, CB + 3)
            global_row(1)
            pe.wait_ge(r_lo, 2 * CB)

            wh2, wl2, wb2 = (w[:].rearrange("p e n -> p (e n)") for w in (wh, wl, wb))

            def experts_of(g):
                _, columns = nc.values_load_multi_w_load_instructions(
                    eid[0:1, bass.ds(4 * g, 4)], engines=(mybir.EngineType.PE,), min_val=0, max_val=(NE - 1) * WC,
                    skip_runtime_bounds_check_because="the chip's own list of experts")
                return columns

            def turn_slots(g, u, bank, count):
                pe.wait_ge(xg_in[u], count)
                for a in range(4):
                    m = nc.tensor.transpose(T[:, bank, a * P:(a + 1) * P], xy[:, u, a], ident[:])
                m.then_inc(t_fill, 1)

            def gate_up(g, u):
                xh, xl = xT[u]
                for a, e in enumerate(experts_of(g)):
                    o = S[:, 2 * u + a // 2, (a % 2) * F2:(a % 2 + 1) * F2]
                    cols = bass.ds(e, F2)
                    nc.tensor.matmul(o, onesr[:], wb2[:, cols], start=True, stop=False)
                    m = three(o, xh[:, a], xl[:, a], wh2[:, cols], wl2[:, cols], start=False)
                m.then_inc(gu_done, 1)

            def turn_gated(g, u, bank):
                pe.wait_ge(ga_ready, g + 1)
                for a in range(4):
                    m = nc.tensor.transpose(T[:, bank, a * P:(a + 1) * P], gu_sb[:, u, 1, a * P:(a + 1) * P], ident[:])
                m.then_inc(t_fill, 1)

            def down(g, u):
                gh, gl = gT[u]
                for a, e in enumerate(experts_of(g)):
                    cols = bass.ds(e + F2, D)
                    o = (O, M)[u][:, a * P:(a + 1) * P]
                    nc.tensor.matmul(o, onesr[:], wb2[:, cols], start=True, stop=False)
                    m = three(o, gh[:, a], gl[:, a], wh2[:, cols], wl2[:, cols], start=False)
                m.then_inc(y_done, 1)

            def expert_step(g, u, count, rows=True, results=True):
                pe.wait_ge(t_lo, rows_fill(g) + 1)
                if rows:
                    turn_slots(g + 1, 1 - u, 0, count)
                gate_up(g, u)
                turn_gated(g - 1, 1 - u, 1 if rows else 0)
                if results:
                    down(g - 2, u)

            pe.wait_ge(w_lo, 4)
            pe.wait_ge(b_in, 16)
            pe.wait_ge(eid_ready, 1)
            pe.wait_ge(g_ready, 2)
            pe.wait_ge(t_lo, T_MOE)
            turn_slots(0, 0, 0, 16)
            turn_slots(1, 1, 1, 16)
            pe.wait_ge(t_lo, rows_fill(0) + 1)
            gate_up(0, 0)
            expert_step(1, 1, 32, results=False)
            expert_step(2, 0, 32)
            expert_step(3, 1, 48)
            with pe.Fori(2, NG // 2 - 1) as j:
                expert_step(2 * j, 0, 16 * (j + 1))
                expert_step(2 * j + 1, 1, 16 * (j + 2))
            expert_step(NG - 2, 0, 16 * (NG // 2))
            expert_step(NG - 1, 1, 0, rows=False)
            pe.wait_ge(up_ready, NG - 1)
            score(TB, 0, 0)
            score(TB, 0, 1)
            pe.wait_ge(t_lo, gated_fill(NG - 2) + 1)
            down(NG - 2, 0)
            turn_gated(NG - 1, 1, 1)
            pe.wait_ge(up_ready, NG)
            score(TB, 0, 2)
            score(TB, 0, 3)
            pe.wait_ge(t_lo, gated_fill(NG - 1) + 1)
            down(NG - 1, 1)

            pe.wait_ge(y_ready, NG)
            attention(1)

        @block.scalar
        def _(act):
            def hi(n, parity, dst, src=None):
                act.wait_ge(t_fill, n + 1)
                nc.scalar.activation(dst, T[:, parity].rearrange("p (a b) -> p a b", a=4), ACT.Copy).then_inc(t_hi, 1)

            act.wait_ge(consts, 9)
            nc.scalar.activation(identr[:], ident[:], ACT.Copy).then_inc(wt_hi, 1)

            def deviation(c):
                act.wait_ge(rstd_in, c + 1)
                nc.scalar.activation(rstd[:, 4 * c:4 * c + 4], mv[:, 4 * c:4 * c + 4, 1], ACT.Sqrt,
                                     bias=epsc[:]).then_inc(rstd_mid, 1)

            def normalise(c):
                act.wait_ge(rstd_ready, c + 1)
                for t in range(4 * c, 4 * c + 4):
                    ins = nc.scalar.activation(xn[:, t], xn[:, t], ACT.Identity, bias=shift[:, t:t + 1],
                                               scale=rstd[:, t:t + 1])
                ins.then_inc(xn_ready[0], 1)

            deviation(0)
            deviation(1)
            normalise(0)
            deviation(2)
            normalise(1)
            act.wait_ge(wt_turned, 1)
            nc.scalar.activation(wspTh[:], S[:, 0, 0:P], ACT.Copy).then_inc(wt_hi, 1)
            nc.scalar.activation(wjTh[:], S[:, 0, P:2 * P], ACT.Copy).then_inc(wt_hi, 1)
            nc.scalar.activation(wglT[:], S[:, 0, 2 * P:3 * P], ACT.Copy).then_inc(wt_hi, 1)
            nc.scalar.activation(wgTh, S[:, 0, 3 * P:3 * P + NE], ACT.Copy).then_inc(wt_hi, 1)

            def spin_hi(b, c):
                act.wait_ge(m_fill, b * CB + c + 1)
                nc.scalar.activation(sTh[:, 512 * c:512 * c + 512], spin_bank(c), ACT.Identity, bias=bspin[:],
                                     accum_out=msum[:, c:c + 1]).then_inc(m_hi, 1)

            def tokens_hi(c, n):
                if 4 <= n < NCH:
                    act.wait_ge(log_done, n - 3)
                hi(n, n % 2, xT[c % 4][0])

            def row_hi(b, c):
                act.wait_ge(r_fill, b * CB + c + 1)
                nc.scalar.activation(sh[:, 4 * c:4 * c + 4], row_bank(b, c).rearrange("p (a b) -> p a b", a=4),
                                     ACT.Copy).then_inc(r_hi, 1)

            def energy_hi(g):
                act.wait_ge(e_fill, g + 1)
                nc.scalar.activation(eTh[:], M[:, 0:2 * P], ACT.Copy, scale=SCALE).then_inc(e_hi, 1)

            tokens_hi(0, 0)
            deviation(3)
            normalise(2)
            tokens_hi(1, 1)
            normalise(3)
            for c in range(NCH):
                if c < CB:
                    spin_hi(0, c)
                if c < 2:
                    tokens_hi(c + 2, c + 2)
                if c < CB:
                    deviation(CB + c)
                if 2 <= c < NCH - 2:
                    tokens_hi(c + 2, c + 2)
                if c == CB:
                    energy_hi(0)
                if c == 1:
                    act.wait_ge(b_adj, 1)
                    nc.scalar.activation(b_hl[0], b_ad, ACT.Copy).then_inc(b_hi, 1)

            def expo(q, half, j):
                nc.scalar.activation(prob[:, half, 512 * j:512 * j + 512], S[:, j], ACT.Exp, bias=nmax[:, half:half + 1],
                                     accum_out=dn2[:, bass.ds(4 * q + j, 1)]).then_inc(exp_done, 1)

            def prob_hi(n, half, j):
                hi(n + j, j % 2, pTh[:, 4 * j:4 * j + 4, half * P:(half + 1) * P])

            def stage(q, half, n):
                for j in range(3):
                    expo(q, half, j + 1)
                    prob_hi(n, half, j)
                prob_hi(n, half, 3)

            dn2 = dn[:].rearrange("p t j -> p (t j)")

            def tanh_step(g):
                act.wait_ge(pre_ready, g + 1)
                nc.scalar.activation(sg[:], sg[:], ACT.Tanh, scale=betac[:]).then_inc(tanh_ready, 1)

            def attention(b):
                q0, g0, n0 = b * TB, b * NP, T_ATT[b]
                if b == 0:
                    act.wait_ge(log_done, NCH)
                    act.wait_ge(b_out, 32)
                    row_hi(0, 0)
                    row_hi(0, 1)
                act.wait_ge(max_ready, q0 + 1)
                expo(q0, 0, 0)
                stage(q0, 0, n0)
                energy_hi(g0 + 1)
                if b == 0:
                    row_hi(0, 2)
                act.wait_ge(max_ready, q0 + 2)
                expo(q0 + 1, 1, 0)
                if b == 0:
                    row_hi(0, 3)

                def pair(i, first=False, last=False):
                    stage(q0 + 2 * i + 1, 1, n0 + 8 * i + 4)
                    if b == 0 and first:
                        global_copy(0)
                    if not first:
                        tanh_step(g0 + i - 1)
                    act.wait_ge(max_ready, q0 + 2 * i + 3)
                    for j in range(4):
                        expo(q0 + 2 * i + 2, 0, j)
                    if b == 0 and isinstance(i, int) and i == 1:
                        act.wait_ge(dlt, 1)
                        nc.scalar.activation(mk[:, 5], mk[:, 4], ACT.Exp).then_inc(exp_dlt, 1)
                    for j in range(3):
                        prob_hi(n0 + 8 * i + 8, 0, j)
                    if not last:
                        energy_hi(g0 + i + 2)
                    act.wait_ge(max_ready, q0 + 2 * i + 4)
                    expo(q0 + 2 * i + 3, 1, 0)
                    act.wait_ge(pv_done, g0 + i + 1)
                    prob_hi(n0 + 8 * i + 8, 0, 3)

                straight = 2 if b == 0 else 1
                for i in range(straight):
                    pair(i, first=i == 0)
                with act.Fori(straight, NP - 2) as i:
                    pair(i)
                pair(NP - 2, last=True)
                i = NP - 1
                stage(q0 + 2 * i + 1, 1, n0 + 8 * i + 4)
                tanh_step(g0 + i - 1)
                tanh_step(g0 + i)

            def global_copy(b):
                act.wait_ge(g_done, b + 1)
                nc.scalar.activation(gb[:], O[:, 0:D], ACT.Copy).then_inc(g_ready, 1)

            attention(0)

            tokens_hi(0, T_PRO_1)
            tokens_hi(1, T_PRO_1 + 1)
            for c in range(CB):
                spin_hi(1, c)
                if c + 2 < CB:
                    tokens_hi(c + 2, T_PRO_1 + c + 2)
            act.wait_ge(sg_ready, NP)
            row_hi(1, 0)
            row_hi(1, 1)
            energy_hi(NP)
            row_hi(1, 2)
            row_hi(1, 3)
            global_copy(1)

            def rows_hi(n, bank, g, u):
                if not (isinstance(g, int) and g < 2):
                    act.wait_ge(gu_done, g - 1)
                hi(n, bank, xT[u][0])

            def gated_hi(n, bank, g, u):
                if not (isinstance(g, int) and g < 2):
                    act.wait_ge(y_done, g - 1)
                hi(n, bank, gT[u][0])

            def sigmoid_half(g, u):
                act.wait_ge(gate_ready, g + 1)
                if not (isinstance(g, int) and g == 0):
                    act.wait_ge(ga_ready, g)
                nc.scalar.activation(th[:], gu_sb[:, u, 0], ACT.Tanh, scale=ALPHA).then_inc(th_ready, 1)

            def y_copy(g, u, stored):
                act.wait_ge(y_done, g + 1)
                if not (isinstance(stored, int) and stored == 0):
                    act.wait_ge(y_out[u], stored)
                nc.scalar.activation(xy[:, 2 + u], (O, M)[u][:].rearrange("p (a d) -> p a d", a=4),
                                     ACT.Copy).then_inc(y_ready, 1)

            rows_hi(T_MOE, 0, 0, 0)
            rows_hi(T_MOE + 1, 1, 1, 1)
            sigmoid_half(0, 0)

            def expert_step(g, u, stored, rows=True, results=True):
                if rows:
                    rows_hi(T_MOE + 2 * g, 0, g + 1, 1 - u)
                gated_hi(T_MOE + 2 * g + (1 if rows else 0), 1 if rows else 0, g - 1, 1 - u)
                sigmoid_half(g, u)
                if results:
                    y_copy(g - 2, u, stored)

            expert_step(1, 1, 0, results=False)
            expert_step(2, 0, 0)
            expert_step(3, 1, 0)
            with act.Fori(2, NG // 2 - 1) as j:
                expert_step(2 * j, 0, 16 * j - 16)
                expert_step(2 * j + 1, 1, 16 * j - 16)
            expert_step(NG - 2, 0, 16 * (NG // 2 - 2))
            expert_step(NG - 1, 1, 16 * (NG // 2 - 2), rows=False)
            y_copy(NG - 2, 0, 16 * (NG // 2 - 1))
            gated_hi(T_MOE + 2 * NG - 1, 1, NG - 1, 1)
            y_copy(NG - 1, 1, 16 * (NG // 2 - 1))

            attention(1)

        @block.vector
        def _(dve):
            v = nc.vector
            count = [0]

            def link(ins):
                count[0] += 1
                ins.then_inc(dchain, 1)
                dve.wait_ge(dchain, count[0])

            def lo(n, parity, dst, high):
                dve.wait_ge(t_hi, n + 1)
                v.tensor_tensor(dst, T[:, parity].rearrange("p (a b) -> p a b", a=4), high.bitcast(F32),
                                ALU.subtract).then_inc(t_lo, 1)

            def spin_lo(b, c):
                dve.wait_ge(m_hi, b * CB + c + 1)
                v.scalar_tensor_tensor(out=sTl[:, 512 * c:512 * c + 512], in0=spin_bank(c), scalar=bspin[:],
                                       in1=sTh[:, 512 * c:512 * c + 512].bitcast(F32), op0=ALU.add,
                                       op1=ALU.subtract).then_inc(m_lo, 1)

            def mean_step(b):
                dve.wait_ge(m_hi, b * CB + CB)
                link(v.tensor_reduce(msum[:, CB:CB + 1], msum[:, 0:CB], AX.X, ALU.add))
                link(v.tensor_scalar(msum[:, CB:CB + 1], msum[:, CB:CB + 1], 1.0 / N, None, ALU.mult))
                v.tensor_scalar(oT[:, 0:P], ident[:], 0.0, msum[:, CB:CB + 1], ALU.mult, ALU.add).then_inc(mean_ready, 1)

            def moments(c):
                dve.wait_ge(ld_x[c], 16)
                for t in range(4 * c, 4 * c + 4):
                    ins = v.bn_stats(stats[:, t], xn[:, t])
                link(ins)
                for t in range(4 * c, 4 * c + 4):
                    ins = v.bn_aggr(mv[:, t], stats[:, t])
                ins.then_inc(rstd_in, 1)

            def inverse(c):
                dve.wait_ge(rstd_mid, c + 1)
                r = rstd[:, 4 * c:4 * c + 4]
                link(v.reciprocal(r, r))
                v.scalar_tensor_tensor(out=shift[:, 4 * c:4 * c + 4], in0=mv[:, 4 * c:4 * c + 4, 0], scalar=-1.0, in1=r,
                                       op0=ALU.mult, op1=ALU.mult).then_inc(rstd_ready, 1)

            def normalise(c):
                dve.wait_ge(rstd_mid, c + 1)
                r = rstd[:, 4 * c:4 * c + 4]
                link(v.reciprocal(r, r))
                for t in range(4 * c, 4 * c + 4):
                    ins = v.tensor_scalar(xn[:, t], xn[:, t], mv[:, t, 0:1], rstd[:, t:t + 1], ALU.subtract, ALU.mult)
                ins.then_inc(xn_ready[1], 1)

            moments(0)
            moments(1)
            inverse(0)
            moments(2)
            inverse(1)
            moments(3)
            inverse(2)
            dve.wait_ge(wt_hi, 5)
            v.tensor_tensor(wspTl[:], S[:, 0, 0:P], wspTh[:].bitcast(F32), ALU.subtract)
            v.tensor_tensor(wjTl[:], S[:, 0, P:2 * P], wjTh[:].bitcast(F32), ALU.subtract)
            v.tensor_tensor(wgTl, S[:, 0, 3 * P:3 * P + NE], wgTh.bitcast(F32), ALU.subtract).then_inc(wt_done, 1)

            def tokens_lo(c, n):
                lo(n, n % 2, xT[c % 4][1], xT[c % 4][0])

            def row_lo(b, c):
                dve.wait_ge(r_hi, b * CB + c + 1)
                v.tensor_tensor(sl[:, 4 * c:4 * c + 4], row_bank(b, c).rearrange("p (a b) -> p a b", a=4),
                                sh[:, 4 * c:4 * c + 4].bitcast(F32), ALU.subtract).then_inc(r_lo, 1)

            def energy_lo(g):
                dve.wait_ge(e_hi, g + 1)
                v.scalar_tensor_tensor(out=eTl[:], in0=M[:, 0:2 * P], scalar=SCALE, in1=eTh[:].bitcast(F32),
                                       op0=ALU.mult, op1=ALU.subtract).then_inc(e_lo, 1)

            def of_batch(w, b):
                return w[:, b * TB:(b + 1) * TB]

            def copy_logits(b):
                dve.wait_ge(log_done, (b + 1) * CB)
                dve.wait_ge(ld_w, 112)
                parts = S[:, 2 + b].rearrange("p (t k e) -> p t k e", k=2, e=NE)
                L = of_batch(LOGIT, b)
                link(v.tensor_tensor(L, parts[:, :, 0], bc(bgr[:], [P, TB, NE], 1), ALU.add))
                v.tensor_tensor(L, L, parts[:, :, 1], ALU.add).then_inc(log_out, 1)

            def best(L, K, top, place):
                sh3 = list(L.shape)
                link(v.tensor_reduce(top, L, AX.X, ALU.max))
                link(v.tensor_tensor(K, L, bc(top, sh3, 2), ALU.is_equal))
                link(v.tensor_tensor(K, K, bc(rev, sh3, 1), ALU.mult))
                link(v.tensor_reduce(place, K, AX.X, ALU.max))

            def first_choice(b):
                dve.wait_ge(log_out, b + 1)
                dve.wait_ge(route_consts, 4)
                place = of_batch(mk[:, 1], b)
                best(of_batch(LOGIT, b), of_batch(KEY, b), of_batch(mk[:, 0], b), place)
                link(v.tensor_tensor(of_batch(OH1, b), of_batch(KEY, b), bc(place, [P, TB, NE], 2), ALU.is_equal))

            def second_choice():
                link(v.scalar_tensor_tensor(out=LOGIT, in0=OH1, scalar=-BIG, in1=LOGIT, op0=ALU.mult, op1=ALU.add))
                best(LOGIT, KEY, mk[:, 2], mk[:, 3])

            tokens_lo(0, 0)
            inverse(3)
            tokens_lo(1, 1)
            for c in range(NCH):
                if c < CB:
                    spin_lo(0, c)
                if c < 2:
                    tokens_lo(c + 2, c + 2)
                if c < CB:
                    moments(CB + c)
                if 1 <= c <= CB:
                    normalise(CB + c - 1)
                if 2 <= c < NCH - 2:
                    tokens_lo(c + 2, c + 2)
                if c == CB:
                    energy_lo(0)
                    mean_step(0)
                if c == CB + 1:
                    copy_logits(0)
                if c == CB + 3:
                    first_choice(0)
                if c == 0:
                    dve.wait_ge(ld_b, 32)
                    pairs = "p (f s) -> p f s"
                    v.tensor_copy(b_ad[:, F2:WC], b_st[:, F2:WC])
                    v.tensor_copy(b_ad[:, 0:F2].rearrange(pairs, s=2)[:, :, 0], b_st[:, 0:F2].rearrange(pairs, s=2)[:, :, 0])
                    v.tensor_scalar(b_ad[:, 0:F2].rearrange(pairs, s=2)[:, :, 1], b_st[:, 0:F2].rearrange(pairs, s=2)[:, :, 1],
                                    1.0, None, ALU.add).then_inc(b_adj, 1)
                if c == 2:
                    dve.wait_ge(b_hi, 1)
                    v.tensor_tensor(b_hl[1], b_ad, b_hl[0].bitcast(F32), ALU.subtract).then_inc(b_lo, 1)

            def choices():
                v.tensor_tensor(mk[:, 4], mk[:, 2], mk[:, 0], ALU.subtract).then_inc(dlt, 1)
                link(v.tensor_tensor(OH2, KEY, bc(mk[:, 3], [P, NT, NE], 2), ALU.is_equal))
                v.tensor_tensor(th[:].bitcast(BF16)[:, 0:NT * NE].rearrange("p (t e) -> p t e", t=NT), OH1, OH2,
                                ALU.add).then_inc(oh_ready, 1)
                dve.wait_ge(rank_fill, 1)
                v.tensor_copy(TOT_E, M[:].rearrange("p (t e) -> p e t", t=NT)).then_inc(rank_out, 1)

            flat = [P, NE, NT]
            by_expert = "p (e t) -> p e t"
            TOT_F, INC_F = bufs[4], bufs[5]
            TOT_E, INC_E, KEY_E = (w.rearrange(by_expert, e=NE) for w in (bufs[4], bufs[5], bufs[1]))

            def expert_starts():
                dve.wait_ge(rank_out, 1)
                link(v.tensor_tensor_scan(INC_F, bufs[6], TOT_F, 0.0, ALU.mult, ALU.add))
                link(v.tensor_copy(small[:, 0], INC_E[:, :, NT - 1]))
                link(v.tensor_tensor(KEY_E, bc(small[:, 0], flat, 2), bc(j128, flat, 1), ALU.is_gt))
                link(v.tensor_reduce(small[:, 1], KEY_E, AX.X, ALU.add))
                link(v.memset(small[:, 2], 1.0))
                link(v.tensor_tensor_scan(ends[:], small[:, 2], small[:, 1], 0.0, ALU.mult, ALU.add))
                link(v.tensor_tensor(small[:, 3], ends[:], small[:, 1], ALU.subtract))
                link(v.tensor_scalar(small[:, 4], small[:, 3], float(P), None, ALU.mult))
                link(v.tensor_tensor(INC_E, INC_E, TOT_E, ALU.subtract))
                link(v.tensor_tensor(INC_E, INC_E, bc(small[:, 4], flat, 2), ALU.add))
                dve.wait_ge(rank_fill, 2)
                v.tensor_copy(LOGIT, M[:].rearrange("p (t e) -> p t e", t=NT)).then_inc(rank_out, 1)

            def slots():
                dve.wait_ge(rank_out, 2)
                link(v.tensor_tensor(LOGIT, LOGIT, INC_E.rearrange("p e t -> p t e"), ALU.add))
                for c, oh in enumerate((OH1, OH2)):
                    link(v.tensor_tensor(KEY, oh, LOGIT, ALU.mult))
                    link(v.tensor_reduce(mk[:, 6], KEY, AX.X, ALU.add))
                    v.tensor_copy(posu[:, c], mk[:, 6]).then_inc(routed, 1)
                    if c == 0:
                        dve.wait_ge(routed, 1)

            def list_experts():
                size = [1, NSLOT_TILES, NE - 1]
                at_or_after = xy[0:1].rearrange("p a b d -> p (a b d)")[:, 0:NSLOT_TILES * (NE - 1)].rearrange(
                    "p (t e) -> p t e", e=NE - 1)
                link(v.tensor_tensor(at_or_after, bc(iot[0:1, :], size, 2), bc(ends[0:1, 0:NE - 1], size, 1), ALU.is_ge))
                link(v.tensor_reduce(count_of[:], at_or_after, AX.X, ALU.add))
                v.tensor_scalar(eid[:], count_of[:], float(WC), None, ALU.mult).then_inc(eid_ready, 1)

            def shares():
                dve.wait_ge(exp_dlt, 1)
                link(v.tensor_scalar(mk[:, 7], mk[:, 5], 1.0, None, ALU.add))
                link(v.reciprocal(w12[:, 0], mk[:, 7]))
                link(v.tensor_tensor(w12[:, 1], w12[:, 0], mk[:, 5], ALU.mult))
                list_experts()

            def bank_max(q, half, j):
                dve.wait_ge(score_done, 4 * q + j + 1)
                return v.tensor_reduce(mx4[:, half, j:j + 1], S[:, j], AX.X, ALU.max)

            def tile_max(q, half):
                dve.wait_ge(max4, q + 1)
                v.tensor_reduce(nmax[:, half:half + 1], mx4[:, half], AX.X, ALU.max, negate=True).then_inc(max_ready, 1)

            def prob_lo(n, half, j):
                cols = slice(half * P, (half + 1) * P)
                lo(n + j, j % 2, pTl[:, 4 * j:4 * j + 4, cols], pTh[:, 4 * j:4 * j + 4, cols])

            def stage(q, half, n):
                for j in range(2):
                    prob_lo(n, half, j)
                    bank_max(q + 1, 1 - half, j)
                bank_max(q + 1, 1 - half, 2)
                bank_max(q + 1, 1 - half, 3).then_inc(max4, 1)
                tile_max(q + 1, 1 - half)
                prob_lo(n, half, 2)

            def out_T(g):
                dve.wait_ge(pv_done, g + 1)
                v.tensor_copy(oT[:], O[:, 0:2 * P]).then_inc(oT_ready, 1)

            def row_sums(q):
                dve.wait_ge(exp_done, 4 * q + 8)
                v.tensor_reduce(den[:], dn[:, bass.ds(q, 2)], AX.X, ALU.add).then_inc(den_ready, 1)

            def invert_sums(g):
                dve.wait_ge(den_ready, 2 * g + 1)
                v.reciprocal(rden[:], den[:]).then_inc(den_ready, 1)

            def combine(g):
                dve.wait_ge(den_ready, 2 * g + 2)
                dve.wait_ge(back_done, g + 1)
                dve.wait_ge(sg_ready, g + 1)
                for a in range(2):
                    ins = v.scalar_tensor_tensor(out=sg[:, a], in0=O[:, (2 + a) * P:(3 + a) * P], scalar=rden[:, a:a + 1],
                                                 in1=sg[:, a], op0=ALU.mult, op1=ALU.add)
                ins.then_inc(pre_ready, 1)

            def add_expert(dst, side, t, c, done):
                for a in range(2):
                    ins = v.scalar_tensor_tensor(out=dst[:, a], in0=xy[:, side, 2 * a + c],
                                                 scalar=w12[:, c, bass.ds(t + a, 1)], in1=dst[:, a],
                                                 op0=ALU.mult, op1=ALU.add)
                ins.then_inc(done, 1)

            def base(b, i):
                if b == 0:
                    return
                if isinstance(i, int) and i == NP - 1:
                    rows_a, rows_b, side = rb_last, xb_last, 2
                    dve.wait_ge(last_in, 32)
                    dve.wait_ge(gat_last, 128)
                else:
                    rows_a, rows_b, side = rb, xb, 0
                    dve.wait_ge(rb_in, 16 * (i + 1))
                    dve.wait_ge(gat_a, 64 * (i + 1))
                add_expert(rows_a, side, 2 * i, 0, ffn_half)
                if side == 0:
                    dve.wait_ge(xb_in, 16 * (i + 1) + 16 * NP)
                    dve.wait_ge(gat_b, 64 * (i + 1))
                add_expert(rows_b, side + 1, 2 * i + TB, 0, ffn_half)
                dve.wait_ge(ffn_half, 2 * i + 1)
                add_expert(rows_a, side, 2 * i, 1, rb_ready)
                dve.wait_ge(ffn_half, 2 * i + 2)
                add_expert(rows_b, side + 1, 2 * i + TB, 1, base_ready)

            def attention(b):
                q0, g0, n0 = b * TB, b * NP, T_ATT[b]
                if b == 0:
                    for j in range(4):
                        ins = bank_max(q0, 0, j)
                    ins.then_inc(max4, 1)
                    tile_max(q0, 0)
                if b == 0:
                    row_lo(0, 0)
                    row_lo(0, 1)
                    first_choice(1)
                stage(q0, 0, n0)
                energy_lo(g0 + 1)
                prob_lo(n0, 0, 3)
                if b == 0:
                    row_lo(0, 2)
                    row_lo(0, 3)

                def pair(i, first=False, last=False, route=None):
                    stage(q0 + 2 * i + 1, 1, n0 + 8 * i + 4)
                    prob_lo(n0 + 8 * i + 4, 1, 3)
                    if not first:
                        base(b, i - 1)
                    if route:
                        route()
                    stage(q0 + 2 * i + 2, 0, n0 + 8 * i + 8)
                    row_sums(q0 + 2 * i)
                    out_T(g0 + i)
                    if not last:
                        energy_lo(g0 + i + 2)
                    invert_sums(g0 + i)
                    prob_lo(n0 + 8 * i + 8, 0, 3)
                    combine(g0 + i)

                routes = (second_choice, choices, expert_starts, slots, shares) if b == 0 else (None,)
                for i, route in enumerate(routes):
                    pair(i, first=i == 0, route=route)
                if len(routes) < NP - 2:
                    with dve.Fori(len(routes), NP - 2) as i:
                        pair(i)
                pair(NP - 2, last=True)
                i = NP - 1
                for j in range(4):
                    prob_lo(n0 + 8 * i + 4, 1, j)
                row_sums(q0 + 2 * i)
                base(b, i - 1)
                base(b, i)
                invert_sums(g0 + i)
                out_T(g0 + i)
                combine(g0 + i)

            copy_logits(1)
            attention(0)

            tokens_lo(0, T_PRO_1)
            tokens_lo(1, T_PRO_1 + 1)
            for c in range(CB):
                spin_lo(1, c)
                if c + 2 < CB:
                    tokens_lo(c + 2, T_PRO_1 + c + 2)
            row_lo(1, 0)
            row_lo(1, 1)
            energy_lo(NP)
            row_lo(1, 2)
            dve.wait_ge(back_done, NP)
            mean_step(1)
            row_lo(1, 3)

            def gate_up(g, u):
                dve.wait_ge(gu_done, g + 1)
                t3 = S[:, 2 * u:2 * u + 2].rearrange("p b (a f s) -> p (b a) f s", a=2, s=2)
                gate, up = (gu_sb[:, u, s].rearrange("p (a f) -> p a f", a=4) for s in range(2))
                v.tensor_scalar(gate, t3[:, :, :, 0], LIMIT, 0.5, ALU.min, ALU.mult).then_inc(gate_ready, 1)
                v.tensor_scalar(up, t3[:, :, :, 1], 1.0 - LIMIT, 1.0 + LIMIT, ALU.max, ALU.min).then_inc(up_ready, 1)

            def gated(g, u):
                dve.wait_ge(th_ready, g + 1)
                dve.wait_ge(au_ready, g + 1)
                v.scalar_tensor_tensor(out=gu_sb[:, u, 1], in0=th[:], scalar=1.0, in1=gu_sb[:, u, 1],
                                       op0=ALU.add, op1=ALU.mult).then_inc(ga_ready, 1)

            def rows_lo(n, bank, u):
                lo(n, bank, xT[u][1], xT[u][0])

            def gated_lo(n, bank, u):
                lo(n, bank, gT[u][1], gT[u][0])

            def expert_step(g, u, rows=True):
                if rows:
                    rows_lo(T_MOE + 2 * g, 0, 1 - u)
                gated(g - 1, 1 - u)
                gate_up(g, u)
                gated_lo(T_MOE + 2 * g + (1 if rows else 0), 1 if rows else 0, 1 - u)

            rows_lo(T_MOE, 0, 0)
            rows_lo(T_MOE + 1, 1, 1)
            gate_up(0, 0)
            expert_step(1, 1)
            with dve.Fori(1, NG // 2 - 1) as j:
                expert_step(2 * j, 0)
                expert_step(2 * j + 1, 1)
            expert_step(NG - 2, 0)
            expert_step(NG - 1, 1, rows=False)
            gated(NG - 1, 1)
            bank_max(TB, 0, 0)
            bank_max(TB, 0, 1)
            gated_lo(T_MOE + 2 * NG - 1, 1, 1)
            bank_max(TB, 0, 2)
            bank_max(TB, 0, 3).then_inc(max4, 1)
            tile_max(TB, 0)

            attention(1)


_INS = ["L0_attn_x", "L0_attn_W_spin", "L0_attn_b_spin", "L0_attn_W_global", "L0_attn_W_J", "L0_attn_beta",
        "L0_ffn_Wg", "L0_ffn_bg", "L0_ffn_Wgu", "L0_ffn_bgu", "L0_ffn_Wd", "L0_ffn_bd"]


def kernel(**inputs):
    import numpy as _np
    import concourse.bacc as _bacc
    from concourse import mybir as _mybir
    from concourse.bass_utils import run_bass_kernel_spmd as _run

    nc = _bacc.Bacc("TRN2", target_bir_lowering=False, num_devices=1)
    arrays, args = {}, []
    for name in _INS:
        a = _np.ascontiguousarray(inputs[name])
        arrays[f"in_{name}"] = a
        args.append(nc.dram_tensor(f"in_{name}", a.shape, _mybir.dt.from_np(a.dtype), kind="ExternalInput").ap())
    shape = inputs["L0_attn_x"].shape
    args.append(nc.dram_tensor("out_y", shape, _mybir.dt.float32, kind="ExternalOutput").ap())
    build(nc, *args)
    r = _run(nc, [arrays], core_ids=[0])
    return r.results[0]["out_y"]
```
